# Optimizing a Trainium2 kernel written in Bass

```python
import numpy as np
import jax
import jax.numpy as jnp

def _softmax(x, axis=-1):
    return jax.nn.softmax(x, axis=axis)

def _gelu(x):
    return jax.nn.gelu(x, approximate=True)

def _silu(x):
    return jax.nn.silu(x)

def _sigmoid(x):
    return jax.nn.sigmoid(x)

def _layernorm(x, axis=-1, eps=1e-05):
    m = jnp.mean(x, axis=axis, keepdims=True)
    v = jnp.var(x, axis=axis, keepdims=True)
    return (x - m) / jnp.sqrt(v + eps)

def _scatter_add(tgt, idx, src, axis=0):
    return tgt.at[idx].add(src)

def _segment_sum(src, seg, n):
    return jax.ops.segment_sum(src, seg, n)
kernel_name = 'mk_xattn_seq_d2_seqx_r2_0ebb34'

def setup_inputs(seed: int=0):
    np.random.seed(seed)
    _w = jnp.asarray

    def _rec_inputs():
        import jax
        import jax.numpy as jnp
        _rk = jax.random.key(seed)
        x = -0.0002928 + 1 * jax.random.normal(jax.random.fold_in(_rk, 1), (4, 2048, 512), jnp.float32)
        _lenS = 2048 - jax.random.randint(jax.random.fold_in(_rk, 7), (4,), 0, max(1, 2048 // 4) + 1, jnp.int32)
        _lenS2 = 77 - jax.random.randint(jax.random.fold_in(_rk, 8), (4,), 0, max(1, 77 // 4) + 1, jnp.int32)
        _ctx_1024P = jax.random.normal(jax.random.fold_in(_rk, 11), (4, 16, 512), jnp.float32)
        _ctx_1024c = jax.random.dirichlet(jax.random.fold_in(_rk, 511), 0.3 * jnp.ones((16,), jnp.float32), (4, 77))
        _ctx_1024t = jnp.einsum('bsk,bkd->bsd', _ctx_1024c, _ctx_1024P)
        _ctx_1024t = _ctx_1024t * jax.lax.rsqrt(jnp.mean(jnp.square(_ctx_1024t)) + 1e-12) * 0.953939
        ctx_1024 = -1.39393e-06 + 0.999914 * (_ctx_1024t + 0.3 * jax.random.normal(jax.random.fold_in(_rk, 611), (4, 77, 512), jnp.float32))
        return (x, ctx_1024)
    x, ctx_1024 = _rec_inputs()

    def _L0_xattn_setup():
        import jax, jax.numpy as jnp
        import numpy as np
        D = 512
        L = 512
        H = 16
        B, T, N = (2, 1024, 1024)

        def layernorm(x, gamma, beta, eps=1e-05):
            mu = jnp.mean(x, axis=-1, keepdims=True)
            var = jnp.var(x, axis=-1, keepdims=True)
            return (x - mu) * jax.lax.rsqrt(var + eps) * gamma + beta
        key = jax.random.key(seed)
        ks = jax.random.split(key, 5)
        x = jax.random.normal(ks[0], (B, T, D), dtype=jnp.float32)
        xf = jax.random.normal(ks[1], (B, N, L), dtype=jnp.float32)
        Wq = jax.random.normal(ks[2], (D, D), dtype=jnp.float32) / np.sqrt(D)
        Wk = jax.random.normal(ks[3], (L, D), dtype=jnp.float32) / np.sqrt(L)
        Wv = jax.random.normal(ks[4], (L, D), dtype=jnp.float32) / np.sqrt(L)
        gamma_x = jnp.ones((D,), jnp.float32)
        beta_x = jnp.zeros((D,), jnp.float32)
        gamma_f = jnp.ones((L,), jnp.float32)
        beta_f = jnp.zeros((L,), jnp.float32)
        return {'x': x, 'xf': xf, 'Wq': Wq, 'Wk': Wk, 'Wv': Wv, 'gamma_x': gamma_x, 'beta_x': beta_x, 'gamma_f': gamma_f, 'beta_f': beta_f}
    _L0_xattn_all = _L0_xattn_setup()
    _L0_xattn_in = {k: v for k, v in _L0_xattn_all.items() if k in ('Wq', 'Wk', 'Wv', 'gamma_x', 'beta_x', 'gamma_f', 'beta_f')}
    del _L0_xattn_all

    def _L1_xattn_setup():
        import jax, jax.numpy as jnp
        import numpy as np
        D_MODEL = 512
        N_HEADS = 16
        D_K = D_MODEL // N_HEADS
        LN_EPS = 1e-05

        def _attention(query, key_value, W_qkv, b_qkv, W_o, b_o, ln_gamma, ln_beta):
            B, Sq, _ = query.shape
            Skv = key_value.shape[1]
            Wq, Wk, Wv = (W_qkv[:D_MODEL], W_qkv[D_MODEL:2 * D_MODEL], W_qkv[2 * D_MODEL:])
            bq, bk, bv = (b_qkv[:D_MODEL], b_qkv[D_MODEL:2 * D_MODEL], b_qkv[2 * D_MODEL:])
            Q = (query @ Wq.T + bq).reshape(B, Sq, N_HEADS, D_K).transpose(0, 2, 1, 3)
            K = (key_value @ Wk.T + bk).reshape(B, Skv, N_HEADS, D_K).transpose(0, 2, 1, 3)
            V = (key_value @ Wv.T + bv).reshape(B, Skv, N_HEADS, D_K).transpose(0, 2, 1, 3)
            scores = jnp.einsum('bhqd,bhkd->bhqk', Q.astype(jnp.float32), K.astype(jnp.float32))
            scores = scores / np.sqrt(D_K)
            attn = jax.nn.softmax(scores, axis=-1)
            context = jnp.einsum('bhqk,bhkd->bhqd', attn, V.astype(jnp.float32)).astype(query.dtype)
            context = context.transpose(0, 2, 1, 3).reshape(B, Sq, D_MODEL)
            output = context @ W_o.T + b_o
            x = output + query
            mu = jnp.mean(x, axis=-1, keepdims=True)
            var = jnp.mean(jnp.square(x - mu), axis=-1, keepdims=True)
            return (x - mu) / jnp.sqrt(var + LN_EPS) * ln_gamma + ln_beta
        key = jax.random.key(seed)
        ks = jax.random.split(key, 8)
        B, Sq, Skv = (2, 1024, 1024)
        scale = 1.0 / np.sqrt(D_MODEL)
        return {'query': jax.random.normal(ks[0], (B, Sq, D_MODEL), dtype=jnp.float32), 'key_value': jax.random.normal(ks[1], (B, Skv, D_MODEL), dtype=jnp.float32), 'W_qkv': jax.random.normal(ks[2], (3 * D_MODEL, D_MODEL), dtype=jnp.float32) * scale, 'b_qkv': jax.random.normal(ks[3], (3 * D_MODEL,), dtype=jnp.float32) * 0.01, 'W_o': jax.random.normal(ks[4], (D_MODEL, D_MODEL), dtype=jnp.float32) * scale, 'b_o': jax.random.normal(ks[5], (D_MODEL,), dtype=jnp.float32) * 0.01, 'ln_gamma': jnp.ones((D_MODEL,), dtype=jnp.float32), 'ln_beta': jnp.zeros((D_MODEL,), dtype=jnp.float32)}
    _L1_xattn_all = _L1_xattn_setup()
    _L1_xattn_in = {k: v for k, v in _L1_xattn_all.items() if k in ('W_qkv', 'b_qkv', 'W_o', 'b_o', 'ln_gamma', 'ln_beta')}
    del _L1_xattn_all
    return {'x': x, 'ctx_1024': ctx_1024, 'L0_xattn_Wq': _L0_xattn_in['Wq'], 'L0_xattn_Wk': _L0_xattn_in['Wk'], 'L0_xattn_Wv': _L0_xattn_in['Wv'], 'L0_xattn_gamma_x': _L0_xattn_in['gamma_x'], 'L0_xattn_beta_x': _L0_xattn_in['beta_x'], 'L0_xattn_gamma_f': _L0_xattn_in['gamma_f'], 'L0_xattn_beta_f': _L0_xattn_in['beta_f'], 'L1_xattn_W_qkv': _L1_xattn_in['W_qkv'], 'L1_xattn_b_qkv': _L1_xattn_in['b_qkv'], 'L1_xattn_W_o': _L1_xattn_in['W_o'], 'L1_xattn_b_o': _L1_xattn_in['b_o'], 'L1_xattn_ln_gamma': _L1_xattn_in['ln_gamma'], 'L1_xattn_ln_beta': _L1_xattn_in['ln_beta']}

def reference(x, ctx_1024, L0_xattn_Wq, L0_xattn_Wk, L0_xattn_Wv, L0_xattn_gamma_x, L0_xattn_beta_x, L0_xattn_gamma_f, L0_xattn_beta_f, L1_xattn_W_qkv, L1_xattn_b_qkv, L1_xattn_W_o, L1_xattn_b_o, L1_xattn_ln_gamma, L1_xattn_ln_beta):
    import jax
    import jax.numpy as jnp

    def _L0_xattn_ref(x, xf, Wq, Wk, Wv, gamma_x, beta_x, gamma_f, beta_f):
        import jax, jax.numpy as jnp
        import numpy as np
        D = 512
        L = 512
        H = 16
        B, T, N = (2, 1024, 1024)

        def layernorm(x, gamma, beta, eps=1e-05):
            mu = jnp.mean(x, axis=-1, keepdims=True)
            var = jnp.var(x, axis=-1, keepdims=True)
            return (x - mu) * jax.lax.rsqrt(var + eps) * gamma + beta
        Bb, Tt, Dd = x.shape
        Nn = xf.shape[1]
        hd = Dd // H
        scale = 1.0 / np.sqrt(hd).astype(np.float32)
        xn = layernorm(x, gamma_x, beta_x)
        fn = layernorm(xf, gamma_f, beta_f)
        q = (xn @ Wq).reshape(Bb, Tt, H, hd)
        k = (fn @ Wk).reshape(Bb, Nn, H, hd)
        v = (fn @ Wv).reshape(Bb, Nn, H, hd)
        attn = jnp.einsum('bthd,bnhd->btnh', q, k) * scale
        w = jax.nn.softmax(attn, axis=2)
        y = jnp.einsum('btnh,bnhd->bthd', w, v).reshape(Bb, Tt, Dd)
        return x + y

    def _L1_xattn_ref(query, key_value, W_qkv, b_qkv, W_o, b_o, ln_gamma, ln_beta):
        import jax, jax.numpy as jnp
        import numpy as np
        D_MODEL = 512
        N_HEADS = 16
        D_K = D_MODEL // N_HEADS
        LN_EPS = 1e-05

        def _attention(query, key_value, W_qkv, b_qkv, W_o, b_o, ln_gamma, ln_beta):
            B, Sq, _ = query.shape
            Skv = key_value.shape[1]
            Wq, Wk, Wv = (W_qkv[:D_MODEL], W_qkv[D_MODEL:2 * D_MODEL], W_qkv[2 * D_MODEL:])
            bq, bk, bv = (b_qkv[:D_MODEL], b_qkv[D_MODEL:2 * D_MODEL], b_qkv[2 * D_MODEL:])
            Q = (query @ Wq.T + bq).reshape(B, Sq, N_HEADS, D_K).transpose(0, 2, 1, 3)
            K = (key_value @ Wk.T + bk).reshape(B, Skv, N_HEADS, D_K).transpose(0, 2, 1, 3)
            V = (key_value @ Wv.T + bv).reshape(B, Skv, N_HEADS, D_K).transpose(0, 2, 1, 3)
            scores = jnp.einsum('bhqd,bhkd->bhqk', Q.astype(jnp.float32), K.astype(jnp.float32))
            scores = scores / np.sqrt(D_K)
            attn = jax.nn.softmax(scores, axis=-1)
            context = jnp.einsum('bhqk,bhkd->bhqd', attn, V.astype(jnp.float32)).astype(query.dtype)
            context = context.transpose(0, 2, 1, 3).reshape(B, Sq, D_MODEL)
            output = context @ W_o.T + b_o
            x = output + query
            mu = jnp.mean(x, axis=-1, keepdims=True)
            var = jnp.mean(jnp.square(x - mu), axis=-1, keepdims=True)
            return (x - mu) / jnp.sqrt(var + LN_EPS) * ln_gamma + ln_beta
        return _attention(query, key_value, W_qkv, b_qkv, W_o, b_o, ln_gamma, ln_beta)
    x = _L0_xattn_ref(x, ctx_1024, L0_xattn_Wq, L0_xattn_Wk, L0_xattn_Wv, L0_xattn_gamma_x, L0_xattn_beta_x, L0_xattn_gamma_f, L0_xattn_beta_f)
    x = _L1_xattn_ref(x, ctx_1024, L1_xattn_W_qkv, L1_xattn_b_qkv, L1_xattn_W_o, L1_xattn_b_o, L1_xattn_ln_gamma, L1_xattn_ln_beta)
    return x

_drawn_inputs = setup_inputs


def setup_inputs(seed=0):
    import zlib

    import numpy as np

    out = dict(_drawn_inputs(seed))
    spreads = {'L0_xattn_gamma_x': (1.0, 0.2),
     'L0_xattn_beta_x': (0.0, 0.553),
     'L0_xattn_gamma_f': (1.0, 0.2),
     'L0_xattn_beta_f': (0.0, 0.1),
     'L1_xattn_ln_gamma': (1.0, 0.2),
     'L1_xattn_ln_beta': (0.0, 0.1)}
    factors = {'L1_xattn_b_qkv': 7.33, 'L1_xattn_b_o': 7.119}
    for name, (base, spread) in spreads.items():
        noise = np.random.default_rng([zlib.crc32(name.encode()), seed]).standard_normal(out[name].shape)
        drawn = base * np.exp(spread * noise) if base else spread * noise
        out[name] = jnp.asarray(drawn.astype(out[name].dtype))
    for name, factor in factors.items():
        out[name] = (out[name] * factor).astype(out[name].dtype)
    return out
```

```python
from contextlib import ExitStack

import numpy as np
import concourse.bass as bass
from concourse import mybir

F32 = mybir.dt.float32
F32R = mybir.dt.float32r
F16 = mybir.dt.float16
ALU = mybir.AluOpType
ACT = mybir.ActivationFunctionType
AX = mybir.AxisListType

P = 128
HI, LO = 0, 1
X0, X1 = 0, 1


class Order:

    def __init__(self, first, middle, last, blocks):
        self.first, self.middle, self.last, self.blocks = first, middle, last, blocks

    def done(self, m, item):
        if isinstance(m, int) and m == 0:
            return self.first.index(item) + 1
        if isinstance(m, int) and m == self.blocks - 1:
            return len(self.first) + len(self.middle) * (m - 1) + self.last.index(item) + 1
        return m * len(self.middle) + (len(self.first) - len(self.middle) + self.middle.index(item) + 1)

    def before(self, m, item):
        n = self.done(m, item) - 1
        return None if isinstance(n, int) and n == 0 else n


def build(nc, x, ctx_in, ctxT_in, wq0, wk0, wv0, gx, bx, gf, bf, w1T, bq1, bk1, bv1, woT, bo, lng, lnb, out):
    B, T, D = x.shape
    C = ctx_in.shape[1]
    H = 16
    HD = D // H
    KC = D // P
    TILES = 4
    ROWS = TILES * P
    BLOCKS = B * T // ROWS
    PER_BATCH = T // ROWS
    UNITS = 2 * TILES
    GH = P // HD
    GK = GH * C
    UK = 2 * GK
    CH = -(-UK // P)
    UP = CH * P
    VW = HD + 1
    EPS = 1e-5
    SCALE = 1.0 / float(np.sqrt(np.float32(HD)))
    BC = B * C

    spans = []
    slot = 0
    for j in range(CH):
        a, b = P * j // C, min(-(-min(P * (j + 1), UK) // C), UK // C)
        spans.append((a, b, slot))
        slot += b - a
    SLOTS = slot
    RENEWALS = GH + 1

    def items(*names):
        return [(n[:-1], int(n[-1])) for n in names]

    head = items("zT0", "zT1", "zT2", "zT3", "qa0", "qa1", "qa2", "qa3")
    attn0_plain = {2: ["xT0"], 4: ["xT1"], 6: ["xT2"]}
    attn0_full = {0: ["cT0", "cT1"], 1: ["cT2", "cT3"], 2: ["wo0"], 3: ["wo1", "xT0"], 4: ["wo2"],
                  5: ["xT1"], 6: [], 7: ["xT2"]}
    tail0_plain = items("xT3", "qb0", "qb1", "qb2", "qb3")
    tail0_full = items("wo3", "xT3", "qb0", "qb1", "qb2", "qb3")
    attn0_plain = {u: items(*attn0_plain.get(u, [])) for u in range(UNITS)}
    attn0_full = {u: items(*attn0_full.get(u, [])) for u in range(UNITS)}
    attn1_full = {u: [head[u]] for u in range(UNITS)}
    attn1_last = {u: [] for u in range(UNITS)}
    end = items("cT0", "cT1", "cT2", "cT3", "wo0", "wo1", "wo2", "wo3")

    def flat(d):
        return [i for u in range(UNITS) for i in d[u]]

    first = [("a" + n, t) for n, t in head] + flat(attn0_plain) + tail0_plain + flat(attn1_full)
    middle = flat(attn0_full) + tail0_full + flat(attn1_full)
    last = flat(attn0_full) + tail0_full + flat(attn1_last) + [("e" + n, t) for n, t in end]
    no_wo = lambda l: [i for i in l if not i[0].endswith("wo")]
    MISC = Order(first, middle, last, BLOCKS)
    SPLIT = Order(no_wo(first), no_wo(middle), no_wo(last), BLOCKS)

    def unit(m, layer, u):
        return m * (2 * UNITS) + (layer * UNITS + u + 1)

    ctx = ExitStack()
    with ctx:
        def sb(name, shape, dt=F32):
            return ctx.enter_context(nc.sbuf_tensor(name, shape, dt))

        def sem(name):
            return ctx.enter_context(nc.semaphore(name))

        scores = ctx.enter_context(nc.psum_tensor("scores", [P, 2, 2, 512], F32))
        turned = ctx.enter_context(nc.psum_tensor("turned", [P, 2, 512], F32))
        heads_out = ctx.enter_context(nc.psum_tensor("heads_out", [P, 512], F32))
        misc = ctx.enter_context(nc.psum_tensor("misc", [P, 512], F32))

        ident = sb("ident", [P, P])
        ones = sb("ones", [P, P])
        w_q0 = [sb(f"w_q0_{i}", [P, KC, D], F32R) for i in range(2)]
        w_q1 = [sb(f"w_q1_{i}", [P, KC, D], F32R) for i in range(2)]
        w_o = [sb(f"w_o_{i}", [P, KC, D], F32R) for i in range(2)]
        k_all = [sb(f"k_all{l}", [P, B, 2, H // GH, C], F16) for l in range(2)]
        v_all = [sb(f"v_all{l}", [P, B, 2, 2 * SLOTS, VW], F16) for l in range(2)]
        k_now = [sb(f"k_now{l}", [P, 2, H // GH, GK], F16) for l in range(2)]
        v_now = [sb(f"v_now{l}", [P, 2, 2 * SLOTS, VW], F16) for l in range(2)]
        cols = sb("cols", [P, 10, KC])
        GX, BX, GF, BF, BQ, BK, BQ0, BKS, ZERO = range(9)
        rows_bc = sb("rows_bc", [P, 3, D])
        xin = sb("xin", [P, TILES, D])
        zc = sb("zc", [P, TILES, D])
        x1 = sb("x1", [P, TILES, D])
        x1b = sb("x1b", [P, TILES, D])
        xT = [sb(f"xT{i}", [P, KC, ROWS], F32R) for i in range(2)]
        cT = [sb(f"cT{i}", [P, KC, ROWS], F32R) for i in range(2)]
        q_all = sb("q_all", [P, 4 * KC * ROWS], F16)
        qT = [[q_all[:, (2 * l + i) * KC * ROWS:(2 * l + i + 1) * KC * ROWS].rearrange("p (k r) -> p k r", k=KC)
               for i in range(2)] for l in range(2)]
        prob = [sb(f"prob{i}", [P, UP]) for i in range(2)]
        probT = [[sb(f"probT{i}{s}", [P, UP], F16) for s in range(2)] for i in range(2)]
        top = sb("top", [P, 2, 8])
        rden = sb("rden", [P, 2, 8])
        stat = sb("stat", [P, TILES, 6])
        mv = sb("mv", [P, TILES, 2])
        rstd = sb("rstd", [P, TILES])
        stat2 = sb("stat2", [P, TILES, 6])
        mv2 = sb("mv2", [P, TILES, 2])
        eps = sb("eps", [P, 1])
        idle_pool = sb("idle_pool", [P, 1])
        idle_dve = sb("idle_dve", [P, 1])
        minus_half = sb("minus_half", [P, 1])
        rstd2 = sb("rstd2", [P, TILES])

        s_w = sem("weights_loaded")
        s_x = [sem(f"x_loaded{t}") for t in range(TILES)]
        s_stored = [sem(f"stored{t}") for t in range(TILES)]
        s_misc = sem("misc_made")
        s_high = sem("high_taken")
        s_low = sem("low_taken")
        s_scores = sem("scores_made")
        s_top = sem("top_found")
        s_sub = sem("top_subtracted")
        s_exp = sem("exp_done")
        s_turned = sem("prob_turned")
        s_phigh = sem("prob_high")
        s_plow = sem("prob_low")
        s_pv = sem("heads_made")
        s_rden = sem("denominator_inverted")
        s_norm = sem("heads_normed")
        s_x1 = sem("x1_made")
        s_x1b = sem("x1_biased")
        s_stat = sem("stats_made")
        s_z = sem("z_made")
        s_stat2 = sem("last_stats_made")
        s_rs = sem("rstd_steps")
        s_rs2 = sem("last_rstd_steps")
        s_fin = sem("result_steps")
        s_kv = [sem(f"kv_now_ready{l}") for l in range(2)]
        s_ctx = sem("context_loaded")
        s_ctxT = sem("turned_context_loaded")
        s_cols = sem("columns_loaded")
        s_rows = sem("broadcast_rows_loaded")
        s_wraw = [sem(f"raw_weights_loaded{i}") for i in range(2)]
        s_clear = sem("cleared")
        s_id = sem("ident_ready")
        s_cstat = sem("context_stats")
        s_cz = sem("context_normalised")
        s_cturn = sem("context_turned")
        s_fn = sem("context_scaled")
        s_fsplit = sem("context_split")
        s_wsplit = sem("weights_split")
        s_kvmade = sem("keys_values_made")
        s_kfull = sem("keys_full")
        s_khigh = sem("keys_high")
        s_klow = sem("keys_low")
        s_vfull = sem("values_full")
        s_vhigh = sem("values_high")
        s_vlow = sem("values_low")
        s_bias0 = sem("query_bias_made")
        s_bq0 = sem("query_bias_taken")
        s_place = sem("values_placed")
        s_crs = sem("context_rstd_steps")
        s_bks = sem("small_columns")

        w_raw = [x1, x1b]
        wkv = cT
        fT = [xT[i][:, :, 0:BC] for i in range(2)]
        craw = xin
        fnT = sb("fnT", [P, KC, BC])
        kf = sb("kf", [P, BC])
        vf = sb("vf", [P, D])
        vst = q_all[:, 0:B * 2 * H * VW].rearrange("p (i h v) -> p i h v", i=2 * B, h=H)
        bv_bc = sb("bv_bc", [P, D])

        x_v = x.rearrange("b (n p) d -> (b n) p d", p=P)
        out_v = out.rearrange("b (n p) d -> (b n) p d", p=P)

        def wview(w):
            return w.rearrange("(k p) n -> p k n", p=P)

        w1v = [w1T[:, i * D:(i + 1) * D].rearrange("(k p) n -> p k n", p=P) for i in range(3)]
        jobs = [(wview(wk0), None, wkv), (wview(wv0), None, wkv), (w1v[1], None, wkv), (w1v[2], None, wkv),
                (wview(wq0), GX, w_q0), (w1v[0], None, w_q1), (wview(woT), None, w_o)]

        def vnow(l, i, half, s, n):
            return v_now[l][:, i, half * SLOTS + s:half * SLOTS + s + n, :]

        block = ctx.enter_context(nc.Block())

        places = []
        for half in range(2):
            for j, (a, b, s) in enumerate(spans):
                for h in range(a, b):
                    lo, hi = max(h * C, P * j), min((h + 1) * C, P * (j + 1))
                    places.append((half, h, s + h - a, lo - h * C, hi - h * C, lo - P * j))

        @block.sync
        def _(sp):
            for b in range(B):
                sp.dma_start(craw[0:C, b, :], ctx_in[b]).then_inc(s_ctx, 16)
            for c, src in enumerate((gx, bx, gf, bf, bq1, bk1)):
                sp.dma_start(cols[:, c, :], src).then_inc(s_cols, 16)
            for n in range(2):
                sp.dma_start(w_raw[n][:], jobs[n][0]).then_inc(s_wraw[n], 16)
            sp.dma_start(bv_bc[:], bv1.partition_broadcast(P)).then_inc(s_rows, 16)
            for c, src in enumerate((bo, lng, lnb)):
                sp.dma_start(rows_bc[:, c, :], src.partition_broadcast(P)).then_inc(s_rows, 16)
            for t in range(TILES):
                sp.wait_ge(s_cz, B)
                sp.dma_start(xin[:, t, :], x_v[t]).then_inc(s_x[t], 16)
            sp.wait_ge(s_wsplit, 2)
            sp.dma_start(w_raw[0][:], jobs[2][0]).then_inc(s_wraw[0], 16)
            sp.wait_ge(s_fsplit, 2)
            sp.dma_start(fnT[:], ctxT_in.rearrange("(k p) n -> p k n", p=P)).then_inc(s_ctxT, 16)

            def place(l):
                sp.wait_ge(s_vhigh, B * (l + 1))
                sp.wait_ge(s_vlow, B * (l + 1))
                for half, h, s, a, b, p0 in places:
                    sp.dma_start(v_all[l][p0:p0 + b - a, :, :, half * SLOTS + s, :].rearrange("p b i v -> p (b i) v"),
                                 vst[a:b, :, half * (H // 2) + h, :]).then_inc(s_place, 16)

            def raw(n):
                sp.wait_ge(s_wsplit, 2 * (n - 1))
                sp.dma_start(w_raw[n % 2][:], jobs[n][0]).then_inc(s_wraw[n % 2], 16)

            raw(3)
            sp.wait_ge(s_clear, 10)
            place(0)
            raw(4)
            raw(5)
            sp.wait_ge(s_bias0, 1)
            raw(6)
            place(1)

            def loads_and_stores(m, more, earlier):
                for t in range(TILES):
                    if more:
                        sp.wait_ge(s_x1, m * TILES + (t + 1))
                        sp.dma_start(xin[:, t, :], x_v[bass.ds(m * TILES + (TILES + t), 1)].squeeze(0)
                                     if not isinstance(m, int) else x_v[m * TILES + TILES + t]).then_inc(s_x[t], 16)
                    if earlier:
                        store(m - 1, t)

            def store(m, t):
                sp.wait_ge(s_fin, m * (3 * TILES) + 3 * (t + 1))
                dst = out_v[m * TILES + t] if isinstance(m, int) else out_v[bass.ds(m * TILES + t, 1)].squeeze(0)
                sp.dma_start(dst, x1b[:, t, :]).then_inc(s_stored[t], 16)

            loads_and_stores(0, True, False)
            with sp.Fori(1, BLOCKS - 1) as m:
                loads_and_stores(m, True, True)
            loads_and_stores(BLOCKS - 1, False, True)
            for t in range(TILES):
                store(BLOCKS - 1, t)
            for t in range(TILES):
                sp.wait_ge(s_stored[t], 16 * BLOCKS)

        @block.gpsimd
        def _(pool):
            pool.memset(ones[:], 1.0).then_inc(s_id, 1)
            pool.wait_ge(s_id, 1)
            pool.affine_select(out=ident[:], in_=ones[:], compare_op=ALU.is_equal, fill=0.0, base=0,
                               pattern=[[-1, P]], channel_multiplier=1).then_inc(s_id, 1)
            for l in range(2):
                pool.memset(v_all[l][:], 0.0).then_inc(s_clear, 1)
                pool.memset(k_now[l][:], 0.0).then_inc(s_clear, 1)
            ones_at = vst[0:C, :, :, HD].rearrange("p (b i) h -> p b i h", i=2)
            pool.memset(ones_at[:, :, HI, :], 1.0).then_inc(s_clear, 1)
            pool.memset(ones_at[:, :, LO, :], 0.0).then_inc(s_clear, 1)
            for i in range(2):
                pool.memset(prob[i][:, UK:UP], 0.0).then_inc(s_clear, 1)
            pool.memset(minus_half[:], -0.5).then_inc(s_clear, 1)
            pool.memset(eps[:], EPS).then_inc(s_clear, 1)
            pool.wait_ge(s_clear, 10)

            def carry_wait():
                pool.tensor_tensor(idle_pool[:], minus_half[:], minus_half[:], ALU.add)

            def inverse_deviation(dst, var, n, signal, before):
                pool.tensor_tensor(dst, var, eps[0:n, :], ALU.add).then_inc(signal, 1)
                pool.wait_ge(signal, before + 1)
                pool.tensor_tensor(dst, dst, minus_half[0:n, :], ALU.pow).then_inc(signal, 1)
                pool.wait_ge(signal, before + 2)
                carry_wait()

            for b in range(B):
                pool.wait_ge(s_cstat, 2 * (b + 1))
                inverse_deviation(rstd[0:C, b:b + 1], mv[0:C, b, 1:2], C, s_crs, 2 * b)
                pool.tensor_scalar(zc[0:C, b, :], craw[0:C, b, :], mv[0:C, b, 0:1], rstd[0:C, b:b + 1],
                                   ALU.subtract, ALU.mult).then_inc(s_cz, 1)

            def normalise(m, t):
                if isinstance(m, int) and m == 1:
                    pool.wait_ge(s_misc, MISC.done(0, ("azT", t)))
                elif not isinstance(m, int) or m:
                    pool.wait_ge(s_misc, MISC.done(m - 1, ("cT", t)))
                pool.wait_ge(s_stat, m * (2 * TILES) + 2 * (t + 1))
                inverse_deviation(rstd[:, t:t + 1], mv[:, t, 1:2], P, s_rs, m * (2 * TILES) + 2 * t)
                if isinstance(m, int) and m == 0:
                    pool.wait_ge(s_cturn, KC)
                pool.tensor_scalar(zc[:, t, :], xin[:, t, :], mv[:, t, 0:1], rstd[:, t:t + 1],
                                   ALU.subtract, ALU.mult).then_inc(s_z, 1)

            def add_x(m, t):
                pool.wait_ge(s_norm, unit(m, 0, 2 * t + 1))
                pool.tensor_tensor(x1[:, t, :], x1[:, t, :], xin[:, t, :], ALU.add).then_inc(s_x1, 1)

            def bias_x1(m, t, earlier):
                pool.wait_ge(s_x1, m * TILES + (t + 1))
                if earlier:
                    pool.wait_ge(s_stored[t], 16 * m)
                pool.tensor_tensor(x1b[:, t, :], x1[:, t, :], rows_bc[:, 0, :], ALU.add).then_inc(s_x1b, 1)

            def finish(m, t):
                pool.wait_ge(s_stat2, m * (2 * TILES) + 2 * (t + 1))
                inverse_deviation(rstd2[:, t:t + 1], mv2[:, t, 1:2], P, s_rs2, m * (2 * TILES) + 2 * t)
                n = m * (3 * TILES) + 3 * t
                r = x1b[:, t, :]
                pool.tensor_scalar(r, r, mv2[:, t, 0:1], rstd2[:, t:t + 1], ALU.subtract, ALU.mult).then_inc(s_fin, 1)
                pool.wait_ge(s_fin, n + 1)
                pool.tensor_tensor(r, r, rows_bc[:, 1, :], ALU.mult).then_inc(s_fin, 1)
                pool.wait_ge(s_fin, n + 2)
                pool.tensor_tensor(r, r, rows_bc[:, 2, :], ALU.add).then_inc(s_fin, 1)

            for t in range(TILES):
                normalise(0, t)

            def one(m, more, earlier):
                order = ([("x", 0), ("f", 0), ("f", 1), ("x", 1), ("f", 2), ("x", 2), ("x", 3), ("f", 3)]
                         if earlier else [("x", t) for t in range(TILES)])
                for what, t in order:
                    if what == "x":
                        add_x(m, t)
                    else:
                        finish(m - 1, t)
                for t in range(TILES):
                    if more:
                        normalise(m + 1, t)
                    bias_x1(m, t, earlier)

            one(0, True, False)
            with pool.Fori(1, BLOCKS - 1) as m:
                one(m, True, True)
            one(BLOCKS - 1, False, True)
            for t in range(TILES):
                finish(BLOCKS - 1, t)

        def project(pe, dst, w, act, g):
            n = 0
            for k in range(KC):
                for a, b in ((HI, HI), (HI, LO), (LO, HI)):
                    mm = pe.matmul(dst, w[a][:, k, g * P:(g + 1) * P], act[b][:, k, :],
                                   start=(n == 0), stop=(n == 3 * KC - 1))
                    n += 1
            return mm

        @block.tensor
        def _(pe):
            pe.wait_ge(s_id, 2)
            pe.wait_ge(s_cz, B)
            for k in range(KC):
                if k >= 1:
                    pe.wait_ge(s_fn, k)
                for b in range(B):
                    mm = pe.transpose(misc[:, b * C:(b + 1) * C], zc[0:C, b, k * P:(k + 1) * P],
                                      ident[0:C, 0:C])
                mm.then_inc(s_cturn, 1)
            for l in range(2):
                pe.wait_ge(s_fsplit, 2 * (l + 1))
                pe.wait_ge(s_wsplit, 4 * l + 2)
                for g in range(KC):
                    if g or not l:
                        if g:
                            pe.wait_ge(s_kfull, KC * l + g)
                    else:
                        pe.wait_ge(s_vfull, B * l)
                    project(pe, misc[:, 0:BC], wkv, fT, g).then_inc(s_kvmade, 1)
                pe.wait_ge(s_wsplit, 4 * l + 4)
                for b in range(B):
                    if b:
                        pe.wait_ge(s_vfull, B * l + b)
                    else:
                        pe.wait_ge(s_kfull, KC * (l + 1))
                    n = 0
                    for k in range(KC):
                        for i, j in ((HI, HI), (HI, LO), (LO, HI)):
                            mm = pe.matmul(misc[0:C, :], fT[i][:, k, b * C:(b + 1) * C], wkv[j][:, k, :],
                                           start=(n == 0), stop=(n == 3 * KC - 1))
                            n += 1
                    mm.then_inc(s_kvmade, 1)
            pe.wait_ge(s_cols, 16 * 6)
            pe.wait_ge(s_wraw[0], 16 * 3)
            pe.wait_ge(s_vfull, 2 * B)
            for g in range(KC):
                for k in range(KC):
                    mm = pe.matmul(misc[:, g:g + 1], w_raw[0][:, k, g * P:(g + 1) * P], cols[:, BX, k:k + 1],
                                   start=(k == 0), stop=(k == KC - 1))
            mm.then_inc(s_bias0, 1)
            pe.wait_ge(s_bq0, 1)
            pe.wait_ge(s_wsplit, 2 * len(jobs))

            turns = {"zT": (zc, s_z), "xT": (x1, s_x1), "cT": (zc, s_norm)}
            projections = {"qa": (w_q0, xT), "qb": (w_q1, xT)}

            def do_misc(m, item, count_m, order_item):
                kind, t = item
                free = MISC.before(count_m, order_item)
                if free is not None:
                    pe.wait_ge(s_low, free)
                if kind in turns:
                    src, ready = turns[kind]
                    pe.wait_ge(ready, unit(m, 1, 2 * t + 1) if kind == "cT" else m * TILES + (t + 1))
                    for k in range(KC):
                        mm = pe.transpose(misc[:, k * P:(k + 1) * P], src[:, t, k * P:(k + 1) * P], ident[:])
                elif kind in projections:
                    w, act = projections[kind]
                    mm = project(pe, misc[:], w, act, t)
                else:
                    n = 0
                    for k in range(KC):
                        for i, j in ((HI, HI), (HI, LO), (LO, HI)):
                            mm = pe.matmul(misc[:], cT[i][:, k, t * P:(t + 1) * P], w_o[j][:, k, :],
                                           start=(n == 0), stop=(n == 3 * KC - 1))
                            n += 1
                mm.then_inc(s_misc, 1)

            def make_scores(m, layer, u):
                t, half = u // 2, u % 2
                n = unit(m, layer, u)
                if not (isinstance(m, int) and m == 0 and layer == 0 and u < 2):
                    pe.wait_ge(s_sub, n - 2)
                q = qT[layer]
                for g in range(2):
                    for r, (i, j) in enumerate(((HI, HI), (HI, LO), (LO, HI))):
                        mm = pe.matmul(scores[:, half, g, 0:GK], q[i][:, 2 * half + g, t * P:(t + 1) * P],
                                       k_now[layer][:, j, 2 * half + g, :], start=(r == 0), stop=(r == 2))
                mm.then_inc(s_scores, 1)

            def turn_prob(m, layer, u):
                n = unit(m, layer, u)
                pe.wait_ge(s_exp, n)
                if not (isinstance(m, int) and m == 0 and layer == 0 and u == 0):
                    pe.wait_ge(s_plow, 2 * n - 2)
                for c in range(CH):
                    mm = pe.transpose(turned[:, c // 3, c % 3 * P:(c % 3 + 1) * P], prob[u % 2][:, c * P:(c + 1) * P], ident[:])
                    if c in (2, CH - 1):
                        mm.then_inc(s_turned, 1)

            def weigh_values(m, layer, u):
                n = unit(m, layer, u)
                if not (isinstance(m, int) and m == 0 and layer == 0 and u == 0):
                    pe.wait_ge(s_norm, n - 1)
                half, y = u % 2, heads_out
                pt = probT
                for c, (a, b, s) in enumerate(spans):
                    if c in (0, 3):
                        pe.wait_ge(s_plow, 2 * n - (1 if c == 0 else 0))
                    for i, j in ((HI, HI), (HI, LO), (LO, HI)):
                        mm = pe.matmul(y[:, a * VW:b * VW], pt[i][u % 2][:, c * P:(c + 1) * P],
                                       vnow(layer, j, half, s, b - a),
                                       start=(c == 0 and i == HI and j == HI),
                                       stop=(c == CH - 1 and i == LO), skip_group_check=True)
                mm.then_inc(s_pv, 1)

            def attend(m, layer, plan, count_m):
                pe.wait_ge(s_kv[layer], m * RENEWALS + RENEWALS)
                make_scores(m, layer, 0)
                make_scores(m, layer, 1)
                for u in range(UNITS):
                    turn_prob(m, layer, u)
                    if u + 2 < UNITS:
                        make_scores(m, layer, u + 2)
                    for item in plan[u]:
                        src_m = m - 1 if item[0] in ("cT", "wo") else m + 1 if item[0] in ("zT", "qa") else m
                        do_misc(src_m, item, m, item)
                    weigh_values(m, layer, u)

            for item in head:
                do_misc(0, item, 0, ("a" + item[0], item[1]))

            def one(m, plan0, tail, plan1):
                pe.wait_ge(s_low, MISC.done(0, ("aqa", KC - 1)) if isinstance(m, int) and m == 0
                           else MISC.done(m - 1, ("qa", KC - 1)))
                attend(m, 0, plan0, m)
                for item in tail:
                    do_misc(m - 1 if item[0] == "wo" else m, item, m, item)
                pe.wait_ge(s_low, MISC.done(m, ("qb", KC - 1)))
                attend(m, 1, plan1, m)

            one(0, attn0_plain, tail0_plain, attn1_full)
            with pe.Fori(1, BLOCKS - 1) as m:
                one(m, attn0_full, tail0_full, attn1_full)
            one(BLOCKS - 1, attn0_full, tail0_full, attn1_last)
            for item in end:
                do_misc(BLOCKS - 1, item, BLOCKS - 1, ("e" + item[0], item[1]))

        targets = {"zT": xT, "xT": xT, "cT": cT}

        def high_low(kind, t, i):
            if kind in targets:
                return targets[kind][i][:, :, t * P:(t + 1) * P], misc[:].rearrange("p (k r) -> p k r", k=KC)
            return qT[0 if kind == "qa" else 1][i][:, t, :], misc[:]

        bias_col = {"qa": BQ0, "qb": BQ}

        @block.scalar
        def _(act):
            for l in range(2):
                for g in range(KC):
                    act.wait_ge(s_kfull, KC * l + g + 1)
                    act.activation(k_all[l][:, :, HI, g, :], kf[:].rearrange("p (b c) -> p b c", b=B),
                                   ACT.Copy).then_inc(s_khigh, 1)
                for b in range(B):
                    act.wait_ge(s_vfull, B * l + b + 1)
                    if l and not b:
                        act.wait_ge(s_place, 16 * len(places))
                    act.activation(vst[0:C, 2 * b + HI, :, 0:HD], vf[0:C, :].rearrange("p (h d) -> p h d", h=H),
                                   ACT.Copy).then_inc(s_vhigh, 1)
            act.wait_ge(s_bq0, 1)
            act.wait_ge(s_place, 2 * 16 * len(places))

            def take_high(count_m, kind, t, order_item):
                act.wait_ge(s_misc, MISC.done(count_m, order_item))
                dst, src = high_low(kind, t, HI)
                if kind in bias_col:
                    act.activation(dst, src, ACT.Identity, bias=cols[:, bias_col[kind], t:t + 1]).then_inc(s_high, 1)
                else:
                    act.activation(dst, src, ACT.Copy).then_inc(s_high, 1)

            def exponent(m, layer, u):
                act.wait_ge(s_sub, unit(m, layer, u))
                p = prob[u % 2][:, 0:UK]
                act.activation(p, p, ACT.Exp).then_inc(s_exp, 1)

            def prob_high(m, layer, u):
                for part, (a, b) in enumerate(((0, 3 * P), (3 * P, UP))):
                    act.wait_ge(s_turned, 2 * unit(m, layer, u) - 1 + part)
                    act.activation(probT[HI][u % 2][:, a:b], turned[:, part, 0:b - a], ACT.Copy).then_inc(s_phigh, 1)

            def attend(m, layer, plan):
                exponent(m, layer, 0)
                for u in range(UNITS):
                    prob_high(m, layer, u)
                    if u + 1 < UNITS:
                        exponent(m, layer, u + 1)
                    for item in plan[u]:
                        if item[0] != "wo":
                            take_high(m, *item, item)

            for kind, t in head:
                take_high(0, kind, t, ("a" + kind, t))

            def one(m, plan0, tail, plan1):
                attend(m, 0, plan0)
                for item in tail:
                    if item[0] != "wo":
                        take_high(m, *item, item)
                attend(m, 1, plan1)

            one(0, attn0_plain, tail0_plain, attn1_full)
            with act.Fori(1, BLOCKS - 1) as m:
                one(m, attn0_full, tail0_full, attn1_full)
            one(BLOCKS - 1, attn0_full, tail0_full, attn1_last)
            for kind, t in end:
                if kind != "wo":
                    take_high(BLOCKS - 1, kind, t, ("e" + kind, t))

        @block.vector
        def _(dve):
            dve.wait_ge(s_ctx, 16 * B)
            for b in range(B):
                dve.bn_stats(stat[0:C, b, :], craw[0:C, b, :]).then_inc(s_cstat, 1)
                dve.wait_ge(s_cstat, 2 * b + 1)
                dve.bn_aggr(mv[0:C, b, :], stat[0:C, b, :]).then_inc(s_cstat, 1)
            dve.wait_ge(s_cols, 16 * 6)
            for k in range(KC):
                dve.wait_ge(s_cturn, k + 1)
                dve.tensor_scalar(fnT[:, k, :], misc[:, 0:BC], cols[:, GF, k:k + 1], cols[:, BF, k:k + 1],
                                  ALU.mult, ALU.add).then_inc(s_fn, 1)

            def split_context(l):
                dve.tensor_copy(fT[HI], fnT[:]).then_inc(s_fsplit, 1)
                dve.wait_ge(s_fsplit, 2 * l + 1)
                dve.tensor_tensor(fT[LO], fnT[:], fT[HI].bitcast(F32), ALU.subtract).then_inc(s_fsplit, 1)

            def split_weights(n):
                _, scale, (high, low) = jobs[n]
                raw = w_raw[n % 2]
                dve.wait_ge(s_wraw[n % 2], 16 * (n // 2 + 1))
                if scale is None:
                    dve.tensor_copy(high[:], raw[:]).then_inc(s_wsplit, 1)
                    dve.wait_ge(s_wsplit, 2 * n + 1)
                    dve.tensor_tensor(low[:], raw[:], high[:].bitcast(F32), ALU.subtract).then_inc(s_wsplit, 1)
                    return
                for k in range(KC):
                    ins = dve.tensor_scalar(high[:, k, :], raw[:, k, :], cols[:, scale, k:k + 1], None, ALU.mult)
                ins.then_inc(s_wsplit, 1)
                dve.wait_ge(s_wsplit, 2 * n + 1)
                for k in range(KC):
                    ins = dve.scalar_tensor_tensor(low[:, k, :], raw[:, k, :], cols[:, scale, k:k + 1],
                                                   high[:, k, :].bitcast(F32), ALU.mult, ALU.subtract)
                ins.then_inc(s_wsplit, 1)

            dve.wait_ge(s_fn, KC)
            split_context(0)
            dve.tensor_scalar(cols[:, BKS, :], cols[:, BK, :], SCALE, None, ALU.mult).then_inc(s_bks, 1)
            dve.memset(cols[:, ZERO, :], 0.0).then_inc(s_bks, 1)
            dve.wait_ge(s_bks, 2)
            split_weights(0)
            for l in range(2):
                for g in range(KC):
                    n = KC * l + g + 1
                    dve.wait_ge(s_kvmade, 2 * KC * l + g + 1)
                    if n > 1:
                        dve.wait_ge(s_klow, n - 1)
                    dve.tensor_scalar(kf[:], misc[:, 0:BC], SCALE, cols[:, BKS if l else ZERO, g:g + 1],
                                      ALU.mult, ALU.add).then_inc(s_kfull, 1)
                    dve.wait_ge(s_kfull, n)
                    dve.wait_ge(s_khigh, n)
                    dve.tensor_tensor(k_all[l][:, :, LO, g, :], kf[:].rearrange("p (b c) -> p b c", b=B),
                                      k_all[l][:, :, HI, g, :], ALU.subtract).then_inc(s_klow, 1)
                split_weights(2 * l + 1)
                for b in range(B):
                    n = B * l + b + 1
                    dve.wait_ge(s_kvmade, 2 * KC * l + KC + b + 1)
                    if n > 1:
                        dve.wait_ge(s_vlow, n - 1)
                    if l:
                        if not b:
                            dve.wait_ge(s_rows, 16 * 4)
                        dve.tensor_tensor(vf[0:C, :], misc[0:C, :], bv_bc[0:C, :], ALU.add).then_inc(s_vfull, 1)
                    else:
                        dve.tensor_copy(vf[0:C, :], misc[0:C, :]).then_inc(s_vfull, 1)
                    dve.wait_ge(s_vfull, n)
                    dve.wait_ge(s_vhigh, n)
                    dve.tensor_tensor(vst[0:C, 2 * b + LO, :, 0:HD], vf[0:C, :].rearrange("p (h d) -> p h d", h=H),
                                      vst[0:C, 2 * b + HI, :, 0:HD], ALU.subtract).then_inc(s_vlow, 1)
                if not l:
                    dve.wait_ge(s_ctxT, 16)
                    split_context(1)
                    split_weights(2)
            split_weights(4)
            dve.wait_ge(s_bias0, 1)
            dve.tensor_copy(cols[:, BQ0, :], misc[:, 0:KC]).then_inc(s_bq0, 1)
            split_weights(5)
            split_weights(6)
            dve.wait_ge(s_bq0, 1)
            dve.wait_ge(s_cz, B)

            def take_low(count_m, kind, t, order_item, src_m):
                if kind == "wo":
                    dve.wait_ge(s_misc, MISC.done(count_m, order_item))
                    dve.wait_ge(s_x1b, src_m * TILES + (t + 1))
                    dve.tensor_tensor(x1b[:, t, :], misc[:], x1b[:, t, :], ALU.add).then_inc(s_low, 1)
                    dve.wait_ge(s_low, MISC.done(count_m, order_item))
                    n = src_m * (2 * TILES) + 2 * t
                    dve.bn_stats(stat2[:, t, :], x1b[:, t, :]).then_inc(s_stat2, 1)
                    dve.wait_ge(s_stat2, n + 1)
                    dve.memset(idle_dve[:], 0.0)
                    dve.bn_aggr(mv2[:, t, :], stat2[:, t, :]).then_inc(s_stat2, 1)
                    return
                dve.wait_ge(s_high, SPLIT.done(count_m, order_item))
                dst, src = high_low(kind, t, LO)
                high, _ = high_low(kind, t, HI)
                if kind in bias_col:
                    dve.scalar_tensor_tensor(dst, src, cols[:, bias_col[kind], t:t + 1], high, ALU.add,
                                             ALU.subtract).then_inc(s_low, 1)
                else:
                    dve.tensor_tensor(dst, src, high.bitcast(F32), ALU.subtract).then_inc(s_low, 1)

            def x_stats(m, t):
                n = m * (2 * TILES) + 2 * t
                dve.wait_ge(s_x[t], 16 * m + 16)
                if not (isinstance(m, int) and m == 0):
                    dve.wait_ge(s_z, (m - 1) * TILES + (t + 1))
                dve.bn_stats(stat[:, t, :], xin[:, t, :]).then_inc(s_stat, 1)
                dve.wait_ge(s_stat, n + 1)
                dve.memset(idle_dve[:], 0.0)
                dve.bn_aggr(mv[:, t, :], stat[:, t, :]).then_inc(s_stat, 1)

            def subtract_top(m, layer, u):
                n = unit(m, layer, u)
                s = scores[:, u % 2, :, 0:GK].rearrange("p g (h c) -> p g h c", c=C)
                mx = top[:, u % 2, :].rearrange("p (g h) -> p g h", g=2)
                dve.wait_ge(s_scores, n)
                dve.tensor_reduce(mx, s, AX.X, ALU.max).then_inc(s_top, 1)
                dve.wait_ge(s_top, n)
                if not (isinstance(m, int) and m == 0 and layer == 0 and u < 2):
                    dve.wait_ge(s_turned, 2 * n - 4)
                dve.tensor_tensor(prob[u % 2][:, 0:UK].rearrange("p (g h c) -> p g h c", g=2, c=C), s,
                                  mx.unsqueeze(3).to_broadcast([P, 2, GH, C]),
                                  ALU.subtract).then_inc(s_sub, 1)

            def prob_low(m, layer, u):
                for part, (a, b) in enumerate(((0, 3 * P), (3 * P, UP))):
                    dve.wait_ge(s_phigh, 2 * unit(m, layer, u) - 1 + part)
                    dve.tensor_tensor(probT[LO][u % 2][:, a:b], turned[:, part, 0:b - a], probT[HI][u % 2][:, a:b],
                                      ALU.subtract).then_inc(s_plow, 1)

            def norm_heads(m, layer, u):
                n = unit(m, layer, u)
                t, half = u // 2, u % 2
                y = heads_out[:, 0:8 * VW].rearrange("p (h v) -> p h v", v=VW)
                dve.wait_ge(s_pv, n)
                dve.reciprocal(rden[:, u % 2, :], y[:, :, HD]).then_inc(s_rden, 1)
                dve.wait_ge(s_rden, n)
                to = (x1, zc)[layer][:, t, half * (D // 2):(half + 1) * (D // 2)]
                if layer == 0 and not (isinstance(m, int) and m == 0):
                    dve.wait_ge(s_x1b, (m - 1) * TILES + (t + 1))
                if layer == 1:
                    at_end = isinstance(m, int) and m == BLOCKS - 1
                    dve.wait_ge(s_misc, MISC.done(m, ("cT" if at_end else "zT", t)))
                dve.tensor_tensor(to.rearrange("p (h d) -> p h d", d=HD), y[:, :, 0:HD],
                                  rden[:, u % 2, :].unsqueeze(2).to_broadcast([P, 8, HD]),
                                  ALU.mult).then_inc(s_norm, 1)

            def renew_kv(m, layer):
                n = m // PER_BATCH
                if not (isinstance(m, int) and m == 0):
                    dve.wait_ge(s_pv, unit(m - 1, layer, UNITS - 1))
                else:
                    dve.wait_ge(s_clear, 10)
                    dve.wait_ge(s_klow, 2 * KC)
                    dve.wait_ge(s_place, 2 * 16 * len(places))
                ks = k_all[layer][:, n] if isinstance(n, int) else k_all[layer][:, bass.ds(n, 1)].squeeze(1)
                vs = v_all[layer][:, n] if isinstance(n, int) else v_all[layer][:, bass.ds(n, 1)].squeeze(1)
                for h in range(GH):
                    r = slice(h * HD, (h + 1) * HD)
                    dve.tensor_copy(k_now[layer][r, :, :, h * C:(h + 1) * C], ks[r]).then_inc(s_kv[layer], 1)
                dve.tensor_copy(v_now[layer][:], vs).then_inc(s_kv[layer], 1)

            def attend(m, layer, plan):
                subtract_top(m, layer, 0)
                for u in range(UNITS):
                    if u >= 1:
                        norm_heads(m, layer, u - 1)
                    prob_low(m, layer, u)
                    if u + 1 < UNITS:
                        subtract_top(m, layer, u + 1)
                    for kind, t in plan[u]:
                        take_low(m, kind, t, (kind, t), m - 1 if kind == "wo" else m)
                norm_heads(m, layer, UNITS - 1)

            renew_kv(0, 0)
            for t in range(TILES):
                x_stats(0, t)
            for kind, t in head:
                take_low(0, kind, t, ("a" + kind, t), 0)

            def one(m, plan0, tail, plan1, more):
                renew_kv(m, 1)
                attend(m, 0, plan0)
                for kind, t in tail:
                    take_low(m, kind, t, (kind, t), m - 1 if kind == "wo" else m)
                if more:
                    renew_kv(m + 1, 0)
                    for t in range(TILES):
                        x_stats(m + 1, t)
                attend(m, 1, plan1)

            one(0, attn0_plain, tail0_plain, attn1_full, True)
            with dve.Fori(1, BLOCKS - 1) as m:
                one(m, attn0_full, tail0_full, attn1_full, True)
            one(BLOCKS - 1, attn0_full, tail0_full, attn1_last, False)
            for kind, t in end:
                take_low(BLOCKS - 1, kind, t, ("e" + kind, t), BLOCKS - 1)


_OUT = ((4, 2048, 512), "float32")


def kernel(x, ctx_1024, L0_xattn_Wq, L0_xattn_Wk, L0_xattn_Wv, L0_xattn_gamma_x, L0_xattn_beta_x,
           L0_xattn_gamma_f, L0_xattn_beta_f, L1_xattn_W_qkv, L1_xattn_b_qkv, L1_xattn_W_o, L1_xattn_b_o,
           L1_xattn_ln_gamma, L1_xattn_ln_beta):
    import concourse.bacc as bacc
    from concourse.bass_utils import run_bass_kernel_spmd

    def column(v):
        return np.ascontiguousarray(np.asarray(v).reshape(4, 128).T)

    c = np.asarray(ctx_1024)
    b = np.asarray(L1_xattn_b_qkv)
    arrays = {
        "x": np.asarray(x), "ctx_rows": c,
        "ctx_turned": np.ascontiguousarray(c.reshape(-1, c.shape[-1]).T),
        "wq0": np.asarray(L0_xattn_Wq), "wk0": np.asarray(L0_xattn_Wk), "wv0": np.asarray(L0_xattn_Wv),
        "gx": column(L0_xattn_gamma_x), "bx": column(L0_xattn_beta_x),
        "gf": column(L0_xattn_gamma_f), "bf": column(L0_xattn_beta_f),
        "w1_turned": np.ascontiguousarray(np.asarray(L1_xattn_W_qkv).T),
        "bq1": column(b[0:512]), "bk1": column(b[512:1024]), "bv1": np.ascontiguousarray(b[1024:1536]),
        "wo_turned": np.ascontiguousarray(np.asarray(L1_xattn_W_o).T),
        "bo": np.asarray(L1_xattn_b_o), "ln_gamma": np.asarray(L1_xattn_ln_gamma),
        "ln_beta": np.asarray(L1_xattn_ln_beta),
    }
    nc = bacc.Bacc("TRN2", target_bir_lowering=False, num_devices=1)
    args = [nc.dram_tensor(n, a.shape, mybir.dt.from_np(a.dtype), kind="ExternalInput").ap()
            for n, a in arrays.items()]
    out = nc.dram_tensor("result", _OUT[0], F32, kind="ExternalOutput").ap()
    build(nc, *args, out)
    return run_bass_kernel_spmd(nc, [arrays], core_ids=[0]).results[0]["result"]
```

```python
from contextlib import ExitStack

import numpy as np
import concourse.bass as bass
from concourse import mybir

F32 = mybir.dt.float32
F32R = mybir.dt.float32r
F16 = mybir.dt.float16
ALU = mybir.AluOpType
ACT = mybir.ActivationFunctionType
AX = mybir.AxisListType

P = 128
HI, LO = 0, 1
X0, X1 = 0, 1


class Order:

    def __init__(self, first, middle, last, blocks):
        self.first, self.middle, self.last, self.blocks = first, middle, last, blocks

    def done(self, m, item):
        if isinstance(m, int) and m == 0:
            return self.first.index(item) + 1
        if isinstance(m, int) and m == self.blocks - 1:
            return len(self.first) + len(self.middle) * (m - 1) + self.last.index(item) + 1
        return m * len(self.middle) + (len(self.first) - len(self.middle) + self.middle.index(item) + 1)

    def before(self, m, item):
        n = self.done(m, item) - 1
        return None if isinstance(n, int) and n == 0 else n


def build(nc, x, ctx_in, ctxT_in, wq0, wk0, wv0, gx, bx, gf, bf, w1T, bq1, bk1, bv1, woT, bo, lng, lnb, out):
    B, T, D = x.shape
    C = ctx_in.shape[1]
    H = 16
    HD = D // H
    KC = D // P
    TILES = 4
    ROWS = TILES * P
    BLOCKS = B * T // ROWS
    PER_BATCH = T // ROWS
    UNITS = 2 * TILES
    GH = P // HD
    GK = GH * C
    UK = 2 * GK
    CH = -(-UK // P)
    UP = CH * P
    VW = HD + 1
    EPS = 1e-5
    SCALE = 1.0 / float(np.sqrt(np.float32(HD)))
    BC = B * C

    spans = []
    slot = 0
    for j in range(CH):
        a, b = P * j // C, min(-(-min(P * (j + 1), UK) // C), UK // C)
        spans.append((a, b, slot))
        slot += b - a
    SLOTS = slot
    RENEWALS = GH + 1

    def items(names):
        return [(n[:-1], int(n[-1])) for n in names.split()]

    def plan(a, b):
        return {u: (items(a.get(u, "")), items(b.get(u, ""))) for u in range(UNITS)}

    head = items("zT0 zT1 zT2 zT3 qa0 qa1 qa2 qa3")
    plan0_first = plan({}, {3: "xT0", 5: "xT1", 7: "xT2"})
    plan0 = plan({0: "cT0", 1: "cT2"}, {0: "cT1", 1: "cT3", 2: "wo0", 3: "xT0", 4: "wo1", 5: "xT1", 7: "xT2"})
    gap_first = items("xT3 qb0 qb1 qb2 qb3")
    gap = items("wo2 xT3 wo3 qb0 qb1 qb2 qb3")
    plan1 = plan({0: "zT0", 1: "zT2"}, {0: "zT1", 1: "zT3", 2: "qa0", 3: "qa1", 4: "qa2", 5: "qa3"})
    plan1_last = plan({}, {})
    end = items("cT0 cT1 cT2 cT3 wo0 wo1 wo2 wo3")

    def flat(d):
        return [i for u in range(UNITS) for part in d[u] for i in part]

    first = [("a" + n, t) for n, t in head] + flat(plan0_first) + gap_first + flat(plan1)
    middle = flat(plan0) + gap + flat(plan1)
    last = flat(plan0) + gap + flat(plan1_last) + [("e" + n, t) for n, t in end]
    no_wo = lambda l: [i for i in l if not i[0].endswith("wo")]
    MISC = Order(first, middle, last, BLOCKS)
    SPLIT = Order(no_wo(first), no_wo(middle), no_wo(last), BLOCKS)

    def unit(m, layer, u):
        return m * (2 * UNITS) + (layer * UNITS + u + 1)

    def is_first(m):
        return isinstance(m, int) and m == 0

    def is_last(m):
        return isinstance(m, int) and m == BLOCKS - 1

    def plans(m):
        return (plan0_first if is_first(m) else plan0, gap_first if is_first(m) else gap,
                plan1_last if is_last(m) else plan1)

    ctx = ExitStack()
    with ctx:
        def sb(name, shape, dt=F32):
            return ctx.enter_context(nc.sbuf_tensor(name, shape, dt))

        def sem(name):
            return ctx.enter_context(nc.semaphore(name))

        scores = ctx.enter_context(nc.psum_tensor("scores", [P, 2, 2, 512], F32))
        turned = ctx.enter_context(nc.psum_tensor("turned", [P, 2, 512], F32))
        heads_out = ctx.enter_context(nc.psum_tensor("heads_out", [P, 512], F32))
        misc = ctx.enter_context(nc.psum_tensor("misc", [P, 512], F32))

        ident = sb("ident", [P, P])
        ones = sb("ones", [P, P])
        w_q0 = [sb(f"w_q0_{i}", [P, KC, D], F32R) for i in range(2)]
        w_q1 = [sb(f"w_q1_{i}", [P, KC, D], F32R) for i in range(2)]
        w_o = [sb(f"w_o_{i}", [P, KC, D], F32R) for i in range(2)]
        k_all = [sb(f"k_all{l}", [P, B, 2, H // GH, C], F16) for l in range(2)]
        v_all = [sb(f"v_all{l}", [P, B, 2, 2 * SLOTS, VW], F16) for l in range(2)]
        k_now = [sb(f"k_now{l}", [P, 2, H // GH, GK], F16) for l in range(2)]
        v_now = [sb(f"v_now{l}", [P, 2, 2 * SLOTS, VW], F16) for l in range(2)]
        cols = sb("cols", [P, 10, KC])
        GX, BX, GF, BF, BQ, BK, BQ0, BKS, ZERO = range(9)
        rows_bc = sb("rows_bc", [P, 3, D])
        xin = sb("xin", [P, TILES, D])
        zc = sb("zc", [P, TILES, D])
        x1 = sb("x1", [P, TILES, D])
        x1b = sb("x1b", [P, TILES, D])
        xT = [sb(f"xT{i}", [P, KC, ROWS], F32R) for i in range(2)]
        cT = [sb(f"cT{i}", [P, KC, ROWS], F32R) for i in range(2)]
        q_all = sb("q_all", [P, 4 * KC * ROWS], F16)
        qT = [[q_all[:, (2 * l + i) * KC * ROWS:(2 * l + i + 1) * KC * ROWS].rearrange("p (k r) -> p k r", k=KC)
               for i in range(2)] for l in range(2)]
        prob = [sb(f"prob{i}", [P, UP]) for i in range(2)]
        probT = [[sb(f"probT{i}{s}", [P, UP], F16) for s in range(2)] for i in range(2)]
        top = sb("top", [P, 2, 8])
        rden = sb("rden", [P, 2, 8])
        stat = sb("stat", [P, TILES, 6])
        mv = sb("mv", [P, TILES, 2])
        rstd = sb("rstd", [P, TILES])
        stat2 = sb("stat2", [P, TILES, 6])
        mv2 = sb("mv2", [P, TILES, 2])
        eps = sb("eps", [P, 1])
        zero = sb("zero", [P, 1])
        idle_dve = sb("idle_dve", [P, 1])
        minus_half = sb("minus_half", [P, 1])
        rstd2 = sb("rstd2", [P, TILES])
        shift = sb("shift", [P, TILES])
        shift2 = sb("shift2", [P, TILES])

        s_w = sem("weights_loaded")
        s_x = [sem(f"x_loaded{t}") for t in range(TILES)]
        s_stored = [sem(f"stored{t}") for t in range(TILES)]
        s_misc = sem("misc_made")
        s_high = sem("high_taken")
        s_low = sem("low_taken")
        s_scores = sem("scores_made")
        s_top = sem("top_found")
        s_sub = sem("top_subtracted")
        s_exp = sem("exp_done")
        s_turned = sem("prob_turned")
        s_phigh = sem("prob_high")
        s_plow = sem("prob_low")
        s_pv = sem("heads_made")
        s_rden = sem("denominator_inverted")
        s_norm = sem("heads_normed")
        s_x1 = sem("x1_made")
        s_x1b = sem("x1_biased")
        s_stat = sem("stats_made")
        s_z = sem("z_made")
        s_stat2 = sem("last_stats_made")
        s_rs = sem("rstd_steps")
        s_rs2 = sem("last_rstd_steps")
        s_applied = sem("last_norm_applied")
        s_fin = sem("result_steps")
        s_kv = [sem(f"kv_now_ready{l}") for l in range(2)]
        s_ctx = sem("context_loaded")
        s_ctxT = sem("turned_context_loaded")
        s_cols = sem("columns_loaded")
        s_rows = sem("broadcast_rows_loaded")
        s_wraw = [sem(f"raw_weights_loaded{i}") for i in range(2)]
        s_clear = sem("cleared")
        s_id = sem("ident_ready")
        s_cstat = sem("context_stats")
        s_cz = sem("context_normalised")
        s_cturn = sem("context_turned")
        s_fn = sem("context_scaled")
        s_fsplit = sem("context_split")
        s_wsplit = sem("weights_split")
        s_kvmade = sem("keys_values_made")
        s_kfull = sem("keys_full")
        s_khigh = sem("keys_high")
        s_klow = sem("keys_low")
        s_vfull = sem("values_full")
        s_vhigh = sem("values_high")
        s_vlow = sem("values_low")
        s_bias0 = sem("query_bias_made")
        s_bq0 = sem("query_bias_taken")
        s_place = sem("values_placed")
        s_crs = sem("context_rstd_steps")
        s_bks = sem("small_columns")

        w_raw = [x1, x1b]
        wkv = cT
        fT = [xT[i][:, :, 0:BC] for i in range(2)]
        craw = xin
        fnT = sb("fnT", [P, KC, BC])
        kf = sb("kf", [P, BC])
        vf = sb("vf", [P, D])
        vst = q_all[:, 0:B * 2 * H * VW].rearrange("p (i h v) -> p i h v", i=2 * B, h=H)
        bv_bc = sb("bv_bc", [P, D])

        x_v = x.rearrange("b (n p) d -> (b n) p d", p=P)
        out_v = out.rearrange("b (n p) d -> (b n) p d", p=P)

        def wview(w):
            return w.rearrange("(k p) n -> p k n", p=P)

        w1v = [w1T[:, i * D:(i + 1) * D].rearrange("(k p) n -> p k n", p=P) for i in range(3)]
        jobs = [(wview(wk0), None, wkv), (wview(wv0), None, wkv), (w1v[1], None, wkv), (w1v[2], None, wkv),
                (wview(wq0), GX, w_q0), (w1v[0], None, w_q1), (wview(woT), None, w_o)]

        def vnow(l, i, half, s, n):
            return v_now[l][:, i, half * SLOTS + s:half * SLOTS + s + n, :]

        block = ctx.enter_context(nc.Block())

        places = []
        for half in range(2):
            for j, (a, b, s) in enumerate(spans):
                for h in range(a, b):
                    lo, hi = max(h * C, P * j), min((h + 1) * C, P * (j + 1))
                    places.append((half, h, s + h - a, lo - h * C, hi - h * C, lo - P * j))

        def bank_of(item, prefix=""):
            turned_bank = {} if prefix else {("wo", 2): 0, ("wo", 3): 1, ("qb", 0): 0, ("qb", 2): 1}
            return turned[:, turned_bank[item], :] if item in turned_bank else misc[:]

        @block.sync
        def _(sp):
            for b in range(B):
                sp.dma_start(craw[0:C, b, :], ctx_in[b]).then_inc(s_ctx, 16)
            for c, src in enumerate((gx, bx, gf, bf, bq1, bk1)):
                sp.dma_start(cols[:, c, :], src).then_inc(s_cols, 16)
            for n in range(2):
                sp.dma_start(w_raw[n][:], jobs[n][0]).then_inc(s_wraw[n], 16)
            sp.dma_start(bv_bc[:], bv1.partition_broadcast(P)).then_inc(s_rows, 16)
            for c, src in enumerate((bo, lng, lnb)):
                sp.dma_start(rows_bc[:, c, :], src.partition_broadcast(P)).then_inc(s_rows, 16)
            for t in range(TILES):
                sp.wait_ge(s_cz, B)
                sp.dma_start(xin[:, t, :], x_v[t]).then_inc(s_x[t], 16)
            sp.wait_ge(s_wsplit, 2)
            sp.dma_start(w_raw[0][:], jobs[2][0]).then_inc(s_wraw[0], 16)
            sp.wait_ge(s_fsplit, 2)
            sp.dma_start(fnT[:], ctxT_in.rearrange("(k p) n -> p k n", p=P)).then_inc(s_ctxT, 16)

            def place(l):
                sp.wait_ge(s_vhigh, B * (l + 1))
                sp.wait_ge(s_vlow, B * (l + 1))
                for half, h, s, a, b, p0 in places:
                    sp.dma_start(v_all[l][p0:p0 + b - a, :, :, half * SLOTS + s, :].rearrange("p b i v -> p (b i) v"),
                                 vst[a:b, :, half * (H // 2) + h, :]).then_inc(s_place, 16)

            def raw(n):
                sp.wait_ge(s_wsplit, 2 * (n - 1))
                sp.dma_start(w_raw[n % 2][:], jobs[n][0]).then_inc(s_wraw[n % 2], 16)

            raw(3)
            sp.wait_ge(s_clear, 11)
            place(0)
            raw(4)
            raw(5)
            sp.wait_ge(s_bias0, 1)
            raw(6)
            place(1)

            def load(m, t):
                sp.wait_ge(s_x1, (m - 1) * TILES + (t + 1))
                src = x_v[m * TILES + t] if isinstance(m, int) else x_v[bass.ds(m * TILES + t, 1)].squeeze(0)
                sp.dma_start(xin[:, t, :], src).then_inc(s_x[t], 16)

            def loads_and_stores(m):
                for what, t in ((load, 0), (store, 0), (load, 1), (store, 1), (load, 2), (load, 3), (store, 2),
                                (store, 3)):
                    if what is load and not is_last(m):
                        load(m + 1, t)
                    if what is store and not is_first(m):
                        store(m - 1, t)

            def store(m, t):
                sp.wait_ge(s_fin, m * (2 * TILES) + 2 * (t + 1))
                dst = out_v[m * TILES + t] if isinstance(m, int) else out_v[bass.ds(m * TILES + t, 1)].squeeze(0)
                sp.dma_start(dst, x1b[:, t, :]).then_inc(s_stored[t], 16)

            loads_and_stores(0)
            with sp.Fori(1, BLOCKS - 1) as m:
                loads_and_stores(m)
            loads_and_stores(BLOCKS - 1)
            for t in range(TILES):
                store(BLOCKS - 1, t)
            for t in range(TILES):
                sp.wait_ge(s_stored[t], 16 * BLOCKS)

        @block.gpsimd
        def _(pool):
            pool.memset(ones[:], 1.0).then_inc(s_id, 1)
            pool.wait_ge(s_id, 1)
            pool.affine_select(out=ident[:], in_=ones[:], compare_op=ALU.is_equal, fill=0.0, base=0,
                               pattern=[[-1, P]], channel_multiplier=1).then_inc(s_id, 1)
            for l in range(2):
                pool.memset(v_all[l][:], 0.0).then_inc(s_clear, 1)
                pool.memset(k_now[l][:], 0.0).then_inc(s_clear, 1)
            ones_at = vst[0:C, :, :, HD].rearrange("p (b i) h -> p b i h", i=2)
            pool.memset(ones_at[:, :, HI, :], 1.0).then_inc(s_clear, 1)
            pool.memset(ones_at[:, :, LO, :], 0.0).then_inc(s_clear, 1)
            for i in range(2):
                pool.memset(prob[i][:, UK:UP], 0.0).then_inc(s_clear, 1)
            pool.memset(minus_half[:], -0.5).then_inc(s_clear, 1)
            pool.memset(eps[:], EPS).then_inc(s_clear, 1)
            pool.memset(zero[:], 0.0).then_inc(s_clear, 1)
            pool.wait_ge(s_clear, 11)

            def inverse_deviation(dst, stats, n, signal, before):
                pool.tensor_tensor(dst, stats[:, 1:2], eps[0:n, :], ALU.add).then_inc(signal, 1)
                pool.wait_ge(signal, before + 1)
                pool.tensor_tensor(dst, dst, minus_half[0:n, :], ALU.pow).then_inc(signal, 1)
                pool.wait_ge(signal, before + 2)

            for b in range(B):
                pool.wait_ge(s_cstat, 2 * (b + 1))
                inverse_deviation(rstd[0:C, b:b + 1], mv[0:C, b, :], C, s_crs, 2 * b)
                pool.tensor_scalar(zc[0:C, b, :], craw[0:C, b, :], mv[0:C, b, 0:1], rstd[0:C, b:b + 1],
                                   ALU.subtract, ALU.mult).then_inc(s_cz, 1)

            def norm_columns(stats, r, sh, t, signal, before):
                inverse_deviation(r[:, t:t + 1], stats[:, t, :], P, signal, before)
                pool.tensor_tensor(sh[:, t:t + 1], stats[:, t, 0:1], r[:, t:t + 1], ALU.mult).then_inc(signal, 1)
                pool.wait_ge(signal, before + 3)
                pool.tensor_tensor(sh[:, t:t + 1], zero[:], sh[:, t:t + 1], ALU.subtract).then_inc(signal, 1)

            def x_columns(m, t):
                pool.wait_ge(s_stat, m * (2 * TILES) + 2 * (t + 1))
                norm_columns(mv, rstd, shift, t, s_rs, m * (4 * TILES) + 4 * t)

            def last_columns(m, t):
                pool.wait_ge(s_stat2, m * (2 * TILES) + 2 * (t + 1))
                norm_columns(mv2, rstd2, shift2, t, s_rs2, m * (4 * TILES) + 4 * t)

            def add_x(m, t):
                pool.wait_ge(s_norm, unit(m, 0, 2 * t + 1))
                pool.tensor_tensor(x1[:, t, :], x1[:, t, :], xin[:, t, :], ALU.add).then_inc(s_x1, 1)

            def bias_x1(m, t, earlier):
                pool.wait_ge(s_x1, m * TILES + (t + 1))
                if earlier:
                    pool.wait_ge(s_stored[t], 16 * m)
                pool.tensor_tensor(x1b[:, t, :], x1[:, t, :], rows_bc[:, 0, :], ALU.add).then_inc(s_x1b, 1)

            def finish(m, t):
                n = m * (2 * TILES) + 2 * t
                r = x1b[:, t, :]
                pool.wait_ge(s_applied, m * TILES + (t + 1))
                pool.tensor_tensor(r, r, rows_bc[:, 1, :], ALU.mult).then_inc(s_fin, 1)
                pool.wait_ge(s_fin, n + 1)
                pool.tensor_tensor(r, r, rows_bc[:, 2, :], ALU.add).then_inc(s_fin, 1)

            for t in range(TILES):
                x_columns(0, t)

            def one(m):
                before = [] if is_first(m) else [(last_columns, 0), (finish, 0), (last_columns, 1), (finish, 1)]
                add_x(m, 0)
                for n in range(1, TILES - 1):
                    for f, t in before[2 * n - 2:2 * n]:
                        f(m - 1, t)
                    add_x(m, n)
                add_x(m, TILES - 1)
                for t in range(TILES):
                    if not is_first(m) and t in (0, 2):
                        last_columns(m - 1, 2 + t // 2)
                    if not is_last(m):
                        x_columns(m + 1, t)
                for t in (2, 3):
                    if not is_first(m):
                        finish(m - 1, t)
                for t in range(TILES):
                    bias_x1(m, t, not is_first(m))

            one(0)
            with pool.Fori(1, BLOCKS - 1) as m:
                one(m)
            one(BLOCKS - 1)
            for t in range(TILES):
                last_columns(BLOCKS - 1, t)
            for t in range(TILES):
                finish(BLOCKS - 1, t)

        def project(pe, dst, w, act, g):
            n = 0
            for k in range(KC):
                for a, b in ((HI, HI), (HI, LO), (LO, HI)):
                    mm = pe.matmul(dst, w[a][:, k, g * P:(g + 1) * P], act[b][:, k, :],
                                   start=(n == 0), stop=(n == 3 * KC - 1))
                    n += 1
            return mm

        @block.tensor
        def _(pe):
            pe.wait_ge(s_id, 2)
            pe.wait_ge(s_cz, B)
            for k in range(KC):
                if k >= 1:
                    pe.wait_ge(s_fn, k)
                for b in range(B):
                    mm = pe.transpose(misc[:, b * C:(b + 1) * C], zc[0:C, b, k * P:(k + 1) * P],
                                      ident[0:C, 0:C])
                mm.then_inc(s_cturn, 1)
            for l in range(2):
                pe.wait_ge(s_fsplit, 2 * (l + 1))
                pe.wait_ge(s_wsplit, 4 * l + 2)
                for g in range(KC):
                    if g or not l:
                        if g:
                            pe.wait_ge(s_kfull, KC * l + g)
                    else:
                        pe.wait_ge(s_vfull, B * l)
                    project(pe, misc[:, 0:BC], wkv, fT, g).then_inc(s_kvmade, 1)
                pe.wait_ge(s_wsplit, 4 * l + 4)
                for b in range(B):
                    if b:
                        pe.wait_ge(s_vfull, B * l + b)
                    else:
                        pe.wait_ge(s_kfull, KC * (l + 1))
                    n = 0
                    for k in range(KC):
                        for i, j in ((HI, HI), (HI, LO), (LO, HI)):
                            mm = pe.matmul(misc[0:C, :], fT[i][:, k, b * C:(b + 1) * C], wkv[j][:, k, :],
                                           start=(n == 0), stop=(n == 3 * KC - 1))
                            n += 1
                    mm.then_inc(s_kvmade, 1)
            pe.wait_ge(s_cols, 16 * 6)
            pe.wait_ge(s_wraw[0], 16 * 3)
            pe.wait_ge(s_vfull, 2 * B)
            for g in range(KC):
                for k in range(KC):
                    mm = pe.matmul(misc[:, g:g + 1], w_raw[0][:, k, g * P:(g + 1) * P], cols[:, BX, k:k + 1],
                                   start=(k == 0), stop=(k == KC - 1))
            mm.then_inc(s_bias0, 1)
            pe.wait_ge(s_bq0, 1)
            pe.wait_ge(s_wsplit, 2 * len(jobs))

            turns = {"zT": (zc, s_z), "xT": (x1, s_x1), "cT": (zc, s_norm)}
            projections = {"qa": (w_q0, xT), "qb": (w_q1, xT)}

            def free_bank(m, item, prefix=""):
                if item[0] == "qb" or item == ("wo", 3) and not prefix:
                    last_of = {0: ("xT", 3), 1: ("xT", 3), 2: ("xT", 3) if is_first(m) else ("wo", 3),
                               3: ("qb", 1)}
                    return None if item[0] == "wo" else MISC.done(m, last_of[item[1]])
                if item == ("xT", 3) and not is_first(m):
                    return MISC.done(m, ("xT", 2))
                if item == ("wo", 2) and not prefix:
                    return None
                return MISC.before(m, (prefix + item[0], item[1]))

            def do_misc(m, item, prefix=""):
                kind, t = item
                bank = bank_of(item, prefix)
                free = free_bank(m, item, prefix)
                if free is not None:
                    pe.wait_ge(s_low, free)
                elif kind == "wo":
                    pe.wait_ge(s_plow, 2 * unit(m, 0, UNITS - 1))
                if kind in turns:
                    src, ready = turns[kind]
                    if kind == "cT":
                        pe.wait_ge(ready, unit(m if prefix else m - 1, 1, 2 * t + 1))
                    elif kind == "zT" and not prefix:
                        pe.wait_ge(ready, m * TILES + (TILES + t + 1))
                    else:
                        pe.wait_ge(ready, m * TILES + (t + 1))
                    for k in range(KC):
                        mm = pe.transpose(bank[:, k * P:(k + 1) * P], src[:, t, k * P:(k + 1) * P], ident[:])
                elif kind in projections:
                    w, act = projections[kind]
                    mm = project(pe, bank, w, act, t)
                else:
                    n = 0
                    for k in range(KC):
                        for i, j in ((HI, HI), (HI, LO), (LO, HI)):
                            mm = pe.matmul(bank, cT[i][:, k, t * P:(t + 1) * P], w_o[j][:, k, :],
                                           start=(n == 0), stop=(n == 3 * KC - 1))
                            n += 1
                mm.then_inc(s_misc, 1)

            def make_scores(m, layer, u):
                t, half = u // 2, u % 2
                n = unit(m, layer, u)
                if u < 2:
                    if layer:
                        pe.wait_ge(s_low, MISC.done(m, ("qb", 2 * u + 1)))
                    else:
                        pe.wait_ge(s_low, MISC.done(0, ("aqa", 2 * u + 1)) if is_first(m) else
                                   MISC.done(m - 1, ("qa", 2 * u + 1)))
                    if u == 0:
                        pe.wait_ge(s_kv[layer], m * RENEWALS + RENEWALS)
                if not (is_first(m) and layer == 0 and u < 2):
                    pe.wait_ge(s_sub, n - 2)
                q = qT[layer]
                for g in range(2):
                    for r, (i, j) in enumerate(((HI, HI), (HI, LO), (LO, HI))):
                        mm = pe.matmul(scores[:, half, g, 0:GK], q[i][:, 2 * half + g, t * P:(t + 1) * P],
                                       k_now[layer][:, j, 2 * half + g, :], start=(r == 0), stop=(r == 2))
                mm.then_inc(s_scores, 1)

            def turn_prob(m, layer, u):
                n = unit(m, layer, u)
                pe.wait_ge(s_exp, n)
                if not (isinstance(m, int) and m == 0 and layer == 0 and u == 0):
                    pe.wait_ge(s_plow, 2 * n - 2)
                if layer == 1 and u == 0:
                    pe.wait_ge(s_low, MISC.done(m, ("qb", 2)))
                for c in range(CH):
                    mm = pe.transpose(turned[:, c // 3, c % 3 * P:(c % 3 + 1) * P], prob[u % 2][:, c * P:(c + 1) * P], ident[:])
                    if c in (2, CH - 1):
                        mm.then_inc(s_turned, 1)

            def weigh_values(m, layer, u):
                n = unit(m, layer, u)
                if not (isinstance(m, int) and m == 0 and layer == 0 and u == 0):
                    pe.wait_ge(s_norm, n - 1)
                half, y = u % 2, heads_out
                pt = probT
                for c, (a, b, s) in enumerate(spans):
                    if c in (0, 3):
                        pe.wait_ge(s_plow, 2 * n - (1 if c == 0 else 0))
                    for i, j in ((HI, HI), (HI, LO), (LO, HI)):
                        mm = pe.matmul(y[:, a * VW:b * VW], pt[i][u % 2][:, c * P:(c + 1) * P],
                                       vnow(layer, j, half, s, b - a),
                                       start=(c == 0 and i == HI and j == HI),
                                       stop=(c == CH - 1 and i == LO), skip_group_check=True)
                mm.then_inc(s_pv, 1)

            for item in head:
                do_misc(0, item, "a")
            make_scores(0, 0, 0)
            make_scores(0, 0, 1)

            def attend(m, layer, steps, earlier):
                for u in range(UNITS):
                    at_a, at_b = steps[u]
                    turn_prob(m, layer, u)
                    for item in at_a:
                        do_misc(m, item)
                    if u:
                        weigh_values(m, layer, u - 1)
                    elif earlier:
                        weigh_values(m - 1, 1, UNITS - 1)
                    if layer == 1 and u == 0:
                        make_scores(m, 1, 1)
                    if u + 2 < UNITS:
                        make_scores(m, layer, u + 2)
                    elif layer == 1 and not is_last(m):
                        make_scores(m + 1, 0, u + 2 - UNITS)
                    for item in at_b:
                        do_misc(m, item)

            def one(m):
                steps0, between, steps1 = plans(m)
                attend(m, 0, steps0, not is_first(m))
                weigh_values(m, 0, UNITS - 1)
                for item in between:
                    if item == ("qb", 3):
                        make_scores(m, 1, 0)
                    do_misc(m, item)
                attend(m, 1, steps1, False)

            one(0)
            with pe.Fori(1, BLOCKS - 1) as m:
                one(m)
            one(BLOCKS - 1)
            weigh_values(BLOCKS - 1, 1, UNITS - 1)
            for item in end:
                do_misc(BLOCKS - 1, item, "e")

        targets = {"zT": xT, "xT": xT, "cT": cT}

        def high_low(item, i, prefix=""):
            kind, t = item
            bank = bank_of(item, prefix)
            if kind in targets:
                return targets[kind][i][:, :, t * P:(t + 1) * P], bank.rearrange("p (k r) -> p k r", k=KC)
            return qT[0 if kind == "qa" else 1][i][:, t, :], bank

        bias_col = {"qa": BQ0, "qb": BQ}

        @block.scalar
        def _(act):
            for l in range(2):
                for g in range(KC):
                    act.wait_ge(s_kfull, KC * l + g + 1)
                    act.activation(k_all[l][:, :, HI, g, :], kf[:].rearrange("p (b c) -> p b c", b=B),
                                   ACT.Copy).then_inc(s_khigh, 1)
                for b in range(B):
                    act.wait_ge(s_vfull, B * l + b + 1)
                    if l and not b:
                        act.wait_ge(s_place, 16 * len(places))
                    act.activation(vst[0:C, 2 * b + HI, :, 0:HD], vf[0:C, :].rearrange("p (h d) -> p h d", h=H),
                                   ACT.Copy).then_inc(s_vhigh, 1)
            act.wait_ge(s_bq0, 1)
            act.wait_ge(s_place, 2 * 16 * len(places))

            def take_high(m, item, prefix=""):
                kind, t = item
                if kind == "wo":
                    return
                act.wait_ge(s_misc, MISC.done(m, (prefix + kind, t)))
                dst, src = high_low(item, HI, prefix)
                if kind in bias_col:
                    act.activation(dst, src, ACT.Identity, bias=cols[:, bias_col[kind], t:t + 1]).then_inc(s_high, 1)
                else:
                    act.activation(dst, src, ACT.Copy).then_inc(s_high, 1)

            def normalise(m, t):
                if isinstance(m, int) and m == 0:
                    act.wait_ge(s_cturn, KC)
                elif isinstance(m, int) and m == 1:
                    act.wait_ge(s_misc, MISC.done(0, ("azT", t)))
                else:
                    act.wait_ge(s_misc, MISC.done(m - 1, ("cT", t)))
                act.wait_ge(s_rs, m * (4 * TILES) + 4 * (t + 1))
                act.activation(zc[:, t, :], xin[:, t, :], ACT.Identity, bias=shift[:, t:t + 1],
                               scale=rstd[:, t:t + 1]).then_inc(s_z, 1)

            def apply_last(m, t):
                act.wait_ge(s_rs2, m * (4 * TILES) + 4 * (t + 1))
                act.activation(x1b[:, t, :], x1b[:, t, :], ACT.Identity, bias=shift2[:, t:t + 1],
                               scale=rstd2[:, t:t + 1]).then_inc(s_applied, 1)

            def renew_kv(m, layer, part):
                n = m // PER_BATCH
                if is_first(m):
                    act.wait_ge(s_clear, 11)
                    act.wait_ge(s_klow, 2 * KC)
                elif part in (0, GH):
                    act.wait_ge(s_pv, unit(m - 1, layer, UNITS - 1))
                a = k_all[layer] if part < GH else v_all[layer]
                src = a[:, n] if isinstance(n, int) else a[:, bass.ds(n, 1)].squeeze(1)
                if part < GH:
                    r = slice(part * HD, (part + 1) * HD)
                    act.activation(k_now[layer][r, :, :, part * C:(part + 1) * C], src[r], ACT.Copy)\
                       .then_inc(s_kv[layer], 1)
                else:
                    act.activation(v_now[layer][:], src, ACT.Copy).then_inc(s_kv[layer], 1)

            def exponent(m, layer, u):
                act.wait_ge(s_sub, unit(m, layer, u))
                p = prob[u % 2][:, 0:UK]
                act.activation(p, p, ACT.Exp).then_inc(s_exp, 1)

            def prob_high(m, layer, u):
                for part, (a, b) in enumerate(((0, 3 * P), (3 * P, UP))):
                    act.wait_ge(s_turned, 2 * unit(m, layer, u) - 1 + part)
                    act.activation(probT[HI][u % 2][:, a:b], turned[:, part, 0:b - a], ACT.Copy).then_inc(s_phigh, 1)

            for part in range(RENEWALS):
                renew_kv(0, 0, part)
            for t in range(TILES):
                normalise(0, t)
            for item in head:
                take_high(0, item, "a")
            exponent(0, 0, 0)

            def one(m):
                steps0, between, steps1 = plans(m)
                for layer, steps in ((0, steps0), (1, steps1)):
                    for u in range(UNITS):
                        if u:
                            for item in steps[u - 1][1]:
                                take_high(m, item)
                        prob_high(m, layer, u)
                        for item in steps[u][0]:
                            take_high(m, item)
                        if u + 1 < UNITS:
                            exponent(m, layer, u + 1)
                        elif layer == 1 and not is_last(m):
                            exponent(m + 1, 0, 0)
                        if 2 <= u < 2 + RENEWALS:
                            if layer == 0:
                                renew_kv(m, 1, u - 2)
                            elif not is_last(m):
                                renew_kv(m + 1, 0, u - 2)
                        if layer == 0 and not is_first(m) and u in (4, 6):
                            apply_last(m - 1, u // 2 - 2)
                    for item in steps[UNITS - 1][1]:
                        take_high(m, item)
                    if layer == 0:
                        for item in between:
                            if item == ("qb", 3):
                                exponent(m, 1, 0)
                            take_high(m, item)
                            if item[0] == "qb" and not is_last(m):
                                normalise(m + 1, item[1])
                            if item[0] == "qb" and item[1] in (1, 3) and not is_first(m):
                                apply_last(m - 1, 2 + item[1] // 2)

            one(0)
            with act.Fori(1, BLOCKS - 1) as m:
                one(m)
            one(BLOCKS - 1)
            for item in end:
                take_high(BLOCKS - 1, item, "e")
            for t in range(TILES):
                apply_last(BLOCKS - 1, t)

        @block.vector
        def _(dve):
            dve.wait_ge(s_ctx, 16 * B)
            for b in range(B):
                dve.bn_stats(stat[0:C, b, :], craw[0:C, b, :]).then_inc(s_cstat, 1)
                dve.wait_ge(s_cstat, 2 * b + 1)
                dve.bn_aggr(mv[0:C, b, :], stat[0:C, b, :]).then_inc(s_cstat, 1)
            dve.wait_ge(s_cols, 16 * 6)
            for k in range(KC):
                dve.wait_ge(s_cturn, k + 1)
                dve.tensor_scalar(fnT[:, k, :], misc[:, 0:BC], cols[:, GF, k:k + 1], cols[:, BF, k:k + 1],
                                  ALU.mult, ALU.add).then_inc(s_fn, 1)

            def split_context(l):
                dve.tensor_copy(fT[HI], fnT[:]).then_inc(s_fsplit, 1)
                dve.wait_ge(s_fsplit, 2 * l + 1)
                dve.tensor_tensor(fT[LO], fnT[:], fT[HI].bitcast(F32), ALU.subtract).then_inc(s_fsplit, 1)

            def split_weights(n):
                _, scale, (high, low) = jobs[n]
                raw = w_raw[n % 2]
                dve.wait_ge(s_wraw[n % 2], 16 * (n // 2 + 1))
                if scale is None:
                    dve.tensor_copy(high[:], raw[:]).then_inc(s_wsplit, 1)
                    dve.wait_ge(s_wsplit, 2 * n + 1)
                    dve.tensor_tensor(low[:], raw[:], high[:].bitcast(F32), ALU.subtract).then_inc(s_wsplit, 1)
                    return
                for k in range(KC):
                    ins = dve.tensor_scalar(high[:, k, :], raw[:, k, :], cols[:, scale, k:k + 1], None, ALU.mult)
                ins.then_inc(s_wsplit, 1)
                dve.wait_ge(s_wsplit, 2 * n + 1)
                for k in range(KC):
                    ins = dve.scalar_tensor_tensor(low[:, k, :], raw[:, k, :], cols[:, scale, k:k + 1],
                                                   high[:, k, :].bitcast(F32), ALU.mult, ALU.subtract)
                ins.then_inc(s_wsplit, 1)

            dve.wait_ge(s_fn, KC)
            split_context(0)
            dve.tensor_scalar(cols[:, BKS, :], cols[:, BK, :], SCALE, None, ALU.mult).then_inc(s_bks, 1)
            dve.memset(cols[:, ZERO, :], 0.0).then_inc(s_bks, 1)
            dve.wait_ge(s_bks, 2)
            split_weights(0)
            for l in range(2):
                for g in range(KC):
                    n = KC * l + g + 1
                    dve.wait_ge(s_kvmade, 2 * KC * l + g + 1)
                    if n > 1:
                        dve.wait_ge(s_klow, n - 1)
                    dve.tensor_scalar(kf[:], misc[:, 0:BC], SCALE, cols[:, BKS if l else ZERO, g:g + 1],
                                      ALU.mult, ALU.add).then_inc(s_kfull, 1)
                    dve.wait_ge(s_kfull, n)
                    dve.wait_ge(s_khigh, n)
                    dve.tensor_tensor(k_all[l][:, :, LO, g, :], kf[:].rearrange("p (b c) -> p b c", b=B),
                                      k_all[l][:, :, HI, g, :], ALU.subtract).then_inc(s_klow, 1)
                split_weights(2 * l + 1)
                for b in range(B):
                    n = B * l + b + 1
                    dve.wait_ge(s_kvmade, 2 * KC * l + KC + b + 1)
                    if n > 1:
                        dve.wait_ge(s_vlow, n - 1)
                    if l:
                        if not b:
                            dve.wait_ge(s_rows, 16 * 4)
                        dve.tensor_tensor(vf[0:C, :], misc[0:C, :], bv_bc[0:C, :], ALU.add).then_inc(s_vfull, 1)
                    else:
                        dve.tensor_copy(vf[0:C, :], misc[0:C, :]).then_inc(s_vfull, 1)
                    dve.wait_ge(s_vfull, n)
                    dve.wait_ge(s_vhigh, n)
                    dve.tensor_tensor(vst[0:C, 2 * b + LO, :, 0:HD], vf[0:C, :].rearrange("p (h d) -> p h d", h=H),
                                      vst[0:C, 2 * b + HI, :, 0:HD], ALU.subtract).then_inc(s_vlow, 1)
                if not l:
                    dve.wait_ge(s_ctxT, 16)
                    split_context(1)
                    split_weights(2)
            split_weights(4)
            dve.wait_ge(s_bias0, 1)
            dve.tensor_copy(cols[:, BQ0, :], misc[:, 0:KC]).then_inc(s_bq0, 1)
            split_weights(5)
            split_weights(6)
            dve.wait_ge(s_bq0, 1)
            dve.wait_ge(s_cz, B)
            dve.wait_ge(s_place, 2 * 16 * len(places))

            def take_low(m, item, prefix=""):
                kind, t = item
                if kind == "wo":
                    b = m if prefix else m - 1
                    dve.wait_ge(s_misc, MISC.done(m, (prefix + kind, t)))
                    dve.wait_ge(s_x1b, b * TILES + (t + 1))
                    dve.tensor_tensor(x1b[:, t, :], bank_of(item, prefix), x1b[:, t, :], ALU.add).then_inc(s_low, 1)
                    dve.wait_ge(s_low, MISC.done(m, (prefix + kind, t)))
                    dve.bn_stats(stat2[:, t, :], x1b[:, t, :]).then_inc(s_stat2, 1)
                    dve.wait_ge(s_stat2, b * (2 * TILES) + (2 * t + 1))
                    dve.memset(idle_dve[:], 0.0)
                    dve.bn_aggr(mv2[:, t, :], stat2[:, t, :]).then_inc(s_stat2, 1)
                    return
                dve.wait_ge(s_high, SPLIT.done(m, (prefix + kind, t)))
                dst, src = high_low(item, LO, prefix)
                high, _ = high_low(item, HI, prefix)
                if kind in bias_col:
                    dve.scalar_tensor_tensor(dst, src, cols[:, bias_col[kind], t:t + 1], high, ALU.add,
                                             ALU.subtract).then_inc(s_low, 1)
                else:
                    dve.tensor_tensor(dst, src, high.bitcast(F32), ALU.subtract).then_inc(s_low, 1)

            def x_stats(m, t):
                n = m * (2 * TILES) + 2 * t
                dve.wait_ge(s_x[t], 16 * m + 16)
                if not (isinstance(m, int) and m == 0):
                    dve.wait_ge(s_z, (m - 1) * TILES + (t + 1))
                dve.bn_stats(stat[:, t, :], xin[:, t, :]).then_inc(s_stat, 1)
                dve.wait_ge(s_stat, n + 1)
                dve.memset(idle_dve[:], 0.0)
                dve.bn_aggr(mv[:, t, :], stat[:, t, :]).then_inc(s_stat, 1)

            def seen_scores(u):
                return scores[:, u % 2, :, 0:GK].rearrange("p g (h c) -> p g h c", c=C), \
                    top[:, u % 2, :].rearrange("p (g h) -> p g h", g=2)

            def find_top(m, layer, u):
                s, mx = seen_scores(u)
                dve.wait_ge(s_scores, unit(m, layer, u))
                dve.tensor_reduce(mx, s, AX.X, ALU.max).then_inc(s_top, 1)

            def subtract_top(m, layer, u):
                n = unit(m, layer, u)
                s, mx = seen_scores(u)
                dve.wait_ge(s_top, n)
                if not (isinstance(m, int) and m == 0 and layer == 0 and u < 2):
                    dve.wait_ge(s_turned, 2 * n - 4)
                dve.tensor_tensor(prob[u % 2][:, 0:UK].rearrange("p (g h c) -> p g h c", g=2, c=C), s,
                                  mx.unsqueeze(3).to_broadcast([P, 2, GH, C]),
                                  ALU.subtract).then_inc(s_sub, 1)

            def prob_low(m, layer, u):
                for part, (a, b) in enumerate(((0, 3 * P), (3 * P, UP))):
                    dve.wait_ge(s_phigh, 2 * unit(m, layer, u) - 1 + part)
                    dve.tensor_tensor(probT[LO][u % 2][:, a:b], turned[:, part, 0:b - a], probT[HI][u % 2][:, a:b],
                                      ALU.subtract).then_inc(s_plow, 1)

            def invert(m, layer, u):
                y = heads_out[:, 0:8 * VW].rearrange("p (h v) -> p h v", v=VW)
                dve.wait_ge(s_pv, unit(m, layer, u))
                dve.reciprocal(rden[:, u % 2, :], y[:, :, HD]).then_inc(s_rden, 1)

            def norm_heads(m, layer, u):
                n = unit(m, layer, u)
                t, half = u // 2, u % 2
                y = heads_out[:, 0:8 * VW].rearrange("p (h v) -> p h v", v=VW)
                dve.wait_ge(s_rden, n)
                to = (x1, zc)[layer][:, t, half * (D // 2):(half + 1) * (D // 2)]
                if layer == 0 and not is_first(m):
                    dve.wait_ge(s_x1b, (m - 1) * TILES + (t + 1))
                if layer == 1:
                    dve.wait_ge(s_misc, MISC.done(m, ("cT" if is_last(m) else "zT", t)))
                dve.tensor_tensor(to.rearrange("p (h d) -> p h d", d=HD), y[:, :, 0:HD],
                                  rden[:, u % 2, :].unsqueeze(2).to_broadcast([P, 8, HD]),
                                  ALU.mult).then_inc(s_norm, 1)

            for t in range(TILES):
                x_stats(0, t)
            for item in head:
                take_low(0, item, "a")
            find_top(0, 0, 0)
            subtract_top(0, 0, 0)

            def attend(m, layer, steps, earlier):
                for u in range(UNITS):
                    ahead = (m, layer, u + 1) if u + 1 < UNITS else (m + 1, 0, 0)
                    has_ahead = u + 1 < UNITS or layer == 1 and not is_last(m)
                    behind = (m, layer, u - 1) if u else (m - 1, 1, UNITS - 1)
                    if has_ahead:
                        find_top(*ahead)
                    if u:
                        for item in steps[u - 1][1]:
                            take_low(m, item)
                    if has_ahead:
                        subtract_top(*ahead)
                    prob_low(m, layer, u)
                    for item in steps[u][0]:
                        take_low(m, item)
                    if u or earlier:
                        invert(*behind)
                        norm_heads(*behind)
                for item in steps[UNITS - 1][1]:
                    take_low(m, item)

            def one(m):
                steps0, between, steps1 = plans(m)
                attend(m, 0, steps0, not is_first(m))
                invert(m, 0, UNITS - 1)
                norm_heads(m, 0, UNITS - 1)
                for item in between:
                    if item == ("qb", 3):
                        find_top(m, 1, 0)
                        subtract_top(m, 1, 0)
                    take_low(m, item)
                    if not is_last(m):
                        if item == ("xT", 3):
                            x_stats(m + 1, 0)
                        if item[0] == "qb" and item[1] < 3:
                            x_stats(m + 1, item[1] + 1)
                attend(m, 1, steps1, False)

            one(0)
            with dve.Fori(1, BLOCKS - 1) as m:
                one(m)
            one(BLOCKS - 1)
            invert(BLOCKS - 1, 1, UNITS - 1)
            norm_heads(BLOCKS - 1, 1, UNITS - 1)
            for item in end:
                take_low(BLOCKS - 1, item, "e")


_OUT = ((4, 2048, 512), "float32")


def kernel(x, ctx_1024, L0_xattn_Wq, L0_xattn_Wk, L0_xattn_Wv, L0_xattn_gamma_x, L0_xattn_beta_x,
           L0_xattn_gamma_f, L0_xattn_beta_f, L1_xattn_W_qkv, L1_xattn_b_qkv, L1_xattn_W_o, L1_xattn_b_o,
           L1_xattn_ln_gamma, L1_xattn_ln_beta):
    import concourse.bacc as bacc
    from concourse.bass_utils import run_bass_kernel_spmd

    def column(v):
        return np.ascontiguousarray(np.asarray(v).reshape(4, 128).T)

    c = np.asarray(ctx_1024)
    b = np.asarray(L1_xattn_b_qkv)
    arrays = {
        "x": np.asarray(x), "ctx_rows": c,
        "ctx_turned": np.ascontiguousarray(c.reshape(-1, c.shape[-1]).T),
        "wq0": np.asarray(L0_xattn_Wq), "wk0": np.asarray(L0_xattn_Wk), "wv0": np.asarray(L0_xattn_Wv),
        "gx": column(L0_xattn_gamma_x), "bx": column(L0_xattn_beta_x),
        "gf": column(L0_xattn_gamma_f), "bf": column(L0_xattn_beta_f),
        "w1_turned": np.ascontiguousarray(np.asarray(L1_xattn_W_qkv).T),
        "bq1": column(b[0:512]), "bk1": column(b[512:1024]), "bv1": np.ascontiguousarray(b[1024:1536]),
        "wo_turned": np.ascontiguousarray(np.asarray(L1_xattn_W_o).T),
        "bo": np.asarray(L1_xattn_b_o), "ln_gamma": np.asarray(L1_xattn_ln_gamma),
        "ln_beta": np.asarray(L1_xattn_ln_beta),
    }
    nc = bacc.Bacc("TRN2", target_bir_lowering=False, num_devices=1)
    args = [nc.dram_tensor(n, a.shape, mybir.dt.from_np(a.dtype), kind="ExternalInput").ap()
            for n, a in arrays.items()]
    out = nc.dram_tensor("result", _OUT[0], F32, kind="ExternalOutput").ap()
    build(nc, *args, out)
    return run_bass_kernel_spmd(nc, [arrays], core_ids=[0]).results[0]["result"]
```

```python
from contextlib import ExitStack

import numpy as np
import concourse.bass as bass
from concourse import mybir

F32 = mybir.dt.float32
F32R = mybir.dt.float32r
F16 = mybir.dt.float16
ALU = mybir.AluOpType
ACT = mybir.ActivationFunctionType
AX = mybir.AxisListType

P = 128
HI, LO = 0, 1
X0, X1 = 0, 1


class Order:

    def __init__(self, in_round, where, first):
        self.in_round, self.where, self.first = in_round, where, first

    def done(self, kind, t, b):
        m = b + self.where[kind, t]
        if isinstance(m, int):
            return sum(len(self.in_round(i)) for i in range(self.first, m)) + self.in_round(m).index((kind, t)) + 1
        n = len(self.in_round(2))
        before = sum(len(self.in_round(i)) for i in range(self.first, 2))
        return m * n + (before - 2 * n + self.in_round(2).index((kind, t)) + 1)

    def before(self, kind, t, b):
        n = self.done(kind, t, b) - 1
        return None if isinstance(n, int) and n == 0 else n


def build(nc, x, ctx_in, ctxT_in, wq0, wk0, wv0, gx, bx, gf, bf, w1T, bq1, bk1, bv1, woT, bo, lng, lnb, out):
    B, T, D = x.shape
    C = ctx_in.shape[1]
    H = 16
    HD = D // H
    KC = D // P
    TILES = 4
    ROWS = TILES * P
    BLOCKS = B * T // ROWS
    PER_BATCH = T // ROWS
    UNITS = 2 * TILES
    GH = P // HD
    GK = GH * C
    UK = 2 * GK
    CH = -(-UK // P)
    UP = CH * P
    VW = HD + 1
    EPS = 1e-5
    SCALE = 1.0 / float(np.sqrt(np.float32(HD)))
    BC = B * C

    spans = []
    slot = 0
    for j in range(CH):
        a, b = P * j // C, min(-(-min(P * (j + 1), UK) // C), UK // C)
        spans.append((a, b, slot))
        slot += b - a
    SLOTS = slot
    RENEWALS = GH + 1

    def is_int(n, top):
        return isinstance(n, int) and n <= top

    plan = {(0, 0): ("cT2", "wo1"), (0, 1): ("xT3", "wo2"), (0, 2): ("cT3", "qb0"), (0, 3): (None, "wo3"),
            (0, 4): (None, "qb1"), (0, 5): (None, "qb2"), (0, 6): (None, "qb3"), (0, 7): ("zT0", "zT1"),
            (1, 0): ("zT2", "zT3"), (1, 1): (None, "qa0"), (1, 2): (None, "qa1"), (1, 3): ("cT0", "qa2"),
            (1, 4): (None, "wo0"), (1, 5): ("cT1", "qa3"), (1, 6): ("xT0", "xT1"), (1, 7): ("xT2", None)}
    plan_0 = {(0, 2): (None, "zT0"), (0, 3): (None, "zT1"), (0, 4): (None, "zT2"), (0, 5): (None, "zT3"),
              (0, 6): (None, "qa0"), (0, 7): (None, "qa1"), (1, 0): (None, "qa2"), (1, 1): (None, "qa3"),
              (1, 2): ("xT0", "xT1"), (1, 3): ("xT2", None)}
    plan_16 = {(0, 0): ("cT2", "wo1"), (0, 1): ("xT3", "cT3"), (0, 2): (None, "qb0"), (0, 3): (None, "qb1"),
               (0, 4): (None, "qb2"), (0, 5): (None, "qb3"), (1, 0): (None, "wo2"), (1, 1): (None, "wo3"),
               (1, 3): ("cT0", None), (1, 4): (None, "wo0"), (1, 5): ("cT1", None)}
    plan_17 = {(0, 0): ("cT2", "wo1"), (0, 1): ("cT3", "wo2"), (0, 2): (None, "wo3")}

    def plan_of(m):
        return {0: plan_0, BLOCKS: plan_16, BLOCKS + 1: plan_17}.get(m, plan) if isinstance(m, int) else plan

    where = {(kind, t): {"zT": -1, "qa": -1, "xT": t // 3, "qb": 1, "cT": 1 + t // 2, "wo": 1 + (t + 2) // 3}[kind]
             for kind in ("zT", "qa", "xT", "qb", "cT", "wo") for t in range(4)}
    FIRST, STEADY = -1, BLOCKS - 2

    def exists(b):
        return not isinstance(b, int) or 0 <= b < BLOCKS

    def item_at(m, layer, u, place):
        name = plan_of(m).get((layer, u), (None, None))[place]
        if name is None:
            return None
        kind, t = name[:-1], int(name[-1])
        b = m - where[kind, t]
        return (kind, t, b) if exists(b) else None

    def items_of_round(m):
        found = [item_at(m, layer, u, place) for layer in range(2) for u in range(UNITS) for place in range(2)]
        return [i[:2] for i in found if i]

    MISC = Order(items_of_round, where, FIRST)
    SPLIT = Order(lambda m: [i for i in items_of_round(m) if i[0] != "wo"], where, FIRST)

    def step_before(m, layer, u):
        return (m, layer, u - 1) if u else (m, 0, UNITS - 1) if layer else (m - 1, 1, UNITS - 1)

    def a_item_before(m, layer, u):
        for _ in range(3):
            m, layer, u = step_before(m, layer, u)
            if item_at(m, layer, u, 0) or not isinstance(m, int):
                return item_at(m, layer, u, 0)
            m, layer, u = step_before(m, layer, u)
        return None

    def in_turned(kind, t, b):
        return isinstance(b, int) and (kind, t, b) in [
            ("zT", 3, 0), ("qa", 1, 0), ("qa", 3, 0), ("qa", 3, 1), ("cT", 3, BLOCKS - 2), ("qb", 1, BLOCKS - 1),
            ("qb", 3, BLOCKS - 1), ("wo", 2, BLOCKS - 1)]

    def last_in_bank(m, layer, u):
        turned_bank = in_turned(*item_at(m, layer, u, 1))
        while not isinstance(m, int) or m >= FIRST:
            m, layer, u = step_before(m, layer, u)
            if turned_bank and unit_at(m, layer, u):
                return None, unit_at(m, layer, u)
            item = item_at(m, layer, u, 1)
            if item and in_turned(*item) == turned_bank:
                return item, None
        return None, None

    def unit(layer, b, u):
        if layer == 0:
            return u + 1 if isinstance(b, int) and b == 0 else b * (2 * UNITS) + (u + 1 - UNITS)
        return b * (2 * UNITS) + (u + 1 + (UNITS if isinstance(b, int) and b == BLOCKS - 1 else 2 * UNITS))

    def unit_at(m, layer, u):
        if u < 0:
            at = (1, m - 2, u + UNITS) if layer == 0 else (0, m, u + UNITS)
        elif u < UNITS:
            at = (layer, m - layer, u)
        else:
            at = (1, m - 1, u - UNITS) if layer == 0 else (0, m + 1, u - UNITS)
        return at if exists(at[1]) else None

    ctx = ExitStack()
    with ctx:
        def sb(name, shape, dt=F32):
            return ctx.enter_context(nc.sbuf_tensor(name, shape, dt))

        def sem(name):
            return ctx.enter_context(nc.semaphore(name))

        scores = ctx.enter_context(nc.psum_tensor("scores", [P, 2, 2, 512], F32))
        turned = ctx.enter_context(nc.psum_tensor("turned", [P, 2, 512], F32))
        heads_out = ctx.enter_context(nc.psum_tensor("heads_out", [P, 512], F32))
        misc = ctx.enter_context(nc.psum_tensor("misc", [P, 512], F32))

        ident = sb("ident", [P, P])
        ones = sb("ones", [P, P])
        w_q0 = [sb(f"w_q0_{i}", [P, KC, D], F32R) for i in range(2)]
        w_q1 = [sb(f"w_q1_{i}", [P, KC, D], F32R) for i in range(2)]
        w_o = [sb(f"w_o_{i}", [P, KC, D], F32R) for i in range(2)]
        k_all = [sb(f"k_all{l}", [P, B, 2, H // GH, C], F16) for l in range(2)]
        v_all = [sb(f"v_all{l}", [P, B, 2, 2 * SLOTS, VW], F16) for l in range(2)]
        k_now = [sb(f"k_now{l}", [P, 2, H // GH, GK], F16) for l in range(2)]
        v_now = [sb(f"v_now{l}", [P, 2, 2 * SLOTS, VW], F16) for l in range(2)]
        cols = sb("cols", [P, 10, KC])
        GX, BX, GF, BF, BQ, BK, BQ0, BKS, ZERO = range(9)
        rows_bc = sb("rows_bc", [P, 3, D])
        xnew = sb("xnew", [P, TILES, D])
        xin = sb("xin", [P, TILES, D])
        zc = sb("zc", [P, TILES, D])
        x1 = sb("x1", [P, TILES, D])
        x1b = sb("x1b", [P, TILES, D])
        xT = [sb(f"xT{i}", [P, KC, ROWS], F32R) for i in range(2)]
        cT = [sb(f"cT{i}", [P, KC, ROWS], F32R) for i in range(2)]
        staging = B * 2 * H * VW
        q_all = sb("q_all", [P, 2 * KC * ROWS + max(2 * KC * ROWS, staging)], F16)
        qT = [[q_all[:, (2 * l + i) * KC * ROWS:(2 * l + i + 1) * KC * ROWS].rearrange("p (k r) -> p k r", k=KC)
               for i in range(2)] for l in range(2)]
        prob_all = sb("prob", [P, 2 * UP])
        prob = [prob_all[:, i * UP:(i + 1) * UP] for i in range(2)]
        probT = [[sb(f"probT{i}{s}", [P, UP], F16) for s in range(2)] for i in range(2)]
        top = sb("top", [P, 2, 8])
        rden = sb("rden", [P, 2, 8])
        stat = sb("stat", [P, TILES, 6])
        mv = sb("mv", [P, TILES, 2])
        rstd = sb("rstd", [P, TILES])
        stat2 = sb("stat2", [P, TILES, 6])
        mv2 = sb("mv2", [P, TILES, 2])
        eps = sb("eps", [P, B])
        zero = sb("zero", [P, B])
        idle_dve = sb("idle_dve", [P, 1])
        minus_half = sb("minus_half", [P, B])
        rstd2 = sb("rstd2", [P, TILES])
        shift = sb("shift", [P, TILES])
        shift2 = sb("shift2", [P, TILES])

        s_w = sem("weights_loaded")
        s_x = [sem(f"x_loaded{t}") for t in range(TILES)]
        s_xin = [sem(f"x_kept{t}") for t in range(TILES)]
        s_stored = [sem(f"stored{t}") for t in range(TILES)]
        s_misc = sem("misc_made")
        s_high = sem("high_taken")
        s_low = sem("low_taken")
        s_scores = sem("scores_made")
        s_top = sem("top_found")
        s_sub = sem("top_subtracted")
        s_exp = sem("exp_done")
        s_turned = sem("prob_turned")
        s_phigh = sem("prob_high")
        s_plow = sem("prob_low")
        s_pv = sem("heads_made")
        s_rden = sem("denominator_inverted")
        s_norm = sem("heads_normed")
        s_x1 = sem("x1_made")
        s_x1b = sem("x1_biased")
        s_stat = sem("stats_made")
        s_z = [sem(f"z_made{t}") for t in range(TILES)]
        s_stat2 = sem("last_stats_made")
        s_rs = sem("rstd_steps")
        s_rs2 = sem("last_rstd_steps")
        s_applied = sem("last_norm_applied")
        s_fin = sem("result_steps")
        s_kv = [sem(f"kv_now_ready{l}") for l in range(2)]
        s_ctx = sem("context_loaded")
        s_ctxT = sem("turned_context_loaded")
        s_cols = sem("columns_loaded")
        s_rows = sem("broadcast_rows_loaded")
        s_wraw = [sem(f"raw_weights_loaded{i}") for i in range(2)]
        s_clear = sem("cleared")
        s_id = sem("ident_ready")
        s_cstat = sem("context_stats")
        s_cz = sem("context_normalised")
        s_cturn = sem("context_turned")
        s_fn = sem("context_scaled")
        s_fsplit = sem("context_split")
        s_whigh = sem("weights_high")
        s_wlow = sem("weights_low")
        s_kvmade = sem("keys_values_made")
        s_kfull = sem("keys_full")
        s_khigh = sem("keys_high")
        s_klow = sem("keys_low")
        s_vfull = sem("values_full")
        s_vhigh = sem("values_high")
        s_vlow = sem("values_low")
        s_bias0 = sem("query_bias_made")
        s_bq0 = sem("query_bias_taken")
        s_place = sem("values_placed")
        s_crs = sem("context_rstd_steps")
        s_bks = sem("small_columns")

        w_raw = [x1, x1b]
        RAW = (0, 1, 0, 1, 0, 1, 1)
        wk, wv = cT, w_o
        fT = [[w_q1[i][:, :, 0:BC] for i in range(2)], [xT[i][:, :, 0:BC] for i in range(2)]]
        craw = xin
        fnT = prob_all[:, 0:KC * BC].rearrange("p (k n) -> p k n", k=KC)
        small = q_all[:, 0:4 * (BC + D)].bitcast(F32)
        kf = [small[:, i * BC:(i + 1) * BC] for i in range(2)]
        vf = [small[:, 2 * BC + i * D:2 * BC + (i + 1) * D] for i in range(2)]
        bv_bc = sb("bv_bc", [P, D])
        vst = q_all[:, 2 * KC * ROWS:2 * KC * ROWS + staging].rearrange("p (i h v) -> p i h v", i=2 * B, h=H)

        x_v = x.rearrange("b (n p) d -> (b n) p d", p=P)
        out_v = out.rearrange("b (n p) d -> (b n) p d", p=P)

        def wview(w):
            return w.rearrange("(k p) n -> p k n", p=P)

        w1v = [w1T[:, i * D:(i + 1) * D].rearrange("(k p) n -> p k n", p=P) for i in range(3)]
        jobs = [(w1v[1], None, wk), (w1v[2], None, wv), (wview(wk0), None, wk), (wview(wv0), None, wv),
                (wview(wq0), GX, w_q0), (w1v[0], None, w_q1), (wview(woT), None, w_o)]
        LAYERS = (1, 0)

        def key_bank(g):
            return scores[:, g // 2, g % 2, :]

        def value_bank(b):
            return (turned[:, 0, :], turned[:, 1, :], heads_out[:], misc[:])[b]

        def vnow(l, i, half, s, n):
            return v_now[l][:, i, half * SLOTS + s:half * SLOTS + s + n, :]

        block = ctx.enter_context(nc.Block())

        places = []
        for j, (a, b, s) in enumerate(spans):
            for h in range(a, b):
                lo, hi = max(h * C, P * j), min((h + 1) * C, P * (j + 1))
                places.append((h, s + h - a, lo - h * C, hi - h * C, lo - P * j))

        def bank_of(kind, t, b):
            steps = plan_of(b + where[kind, t]).items()
            u = next((u for (_, u), (at_a, _) in steps if at_a == f"{kind}{t}"), None)
            if u is not None:
                return scores[:, (u + 1) % 2, 0, :]
            return turned[:, 1, :] if in_turned(kind, t, b) else misc[:]

        @block.sync
        def _(sp):
            def raw(n):
                earlier = [i for i in range(n) if RAW[i] == RAW[n]]
                if earlier:
                    sp.wait_ge(s_wlow, earlier[-1] + 1)
                sp.dma_start(w_raw[RAW[n]][:], jobs[n][0]).then_inc(s_wraw[RAW[n]], 16)

            sp.dma_start(fnT, ctxT_in.rearrange("(k p) n -> p k n", p=P)).then_inc(s_ctxT, 16)
            raw(0)
            sp.dma_start(craw[0:C, :, :], ctx_in.rearrange("b c d -> c b d")).then_inc(s_ctx, 16)
            raw(1)
            for c, src in enumerate((gx, bx, gf, bf, bq1, bk1)):
                sp.dma_start(cols[:, c, :], src).then_inc(s_cols, 16)
            sp.dma_start(bv_bc[:], bv1.partition_broadcast(P)).then_inc(s_rows, 16)
            for t in range(TILES):
                sp.dma_start(xnew[:, t, :], x_v[t]).then_inc(s_x[t], 16)
            raw(2)
            raw(3)

            def place(q):
                sp.wait_ge(s_vhigh, B * (q + 1))
                sp.wait_ge(s_vlow, B * (q + 1))
                v = v_all[LAYERS[q]][:].rearrange("p b i (half s) v -> p (b i) half s v", half=2)
                src = vst.rearrange("p i (half h) v -> p i half h v", half=2)
                for h, s, a, b, p0 in places:
                    sp.dma_start(v[p0:p0 + b - a, :, :, s, :], src[a:b, :, :, h, :]).then_inc(s_place, 16)

            sp.wait_ge(s_clear, 9)
            raw(4)
            place(0)
            raw(5)
            place(1)
            for c, src in enumerate((bo, lng, lnb)):
                sp.dma_start(rows_bc[:, c, :], src.partition_broadcast(P)).then_inc(s_rows, 16)

            def load(b, t):
                if not exists(b):
                    return
                src = x_v[b * TILES + t] if isinstance(b, int) else x_v[bass.ds(b * TILES + t, 1)].squeeze(0)
                blocks = b * 16
                sp.wait_ge(s_xin[t], blocks)
                sp.wait_ge(s_z[t], blocks)
                sp.dma_start(xnew[:, t, :], src).then_inc(s_x[t], 16)

            def keep(b, t):
                if not exists(b):
                    return
                if exists(b - 1):
                    sp.wait_ge(s_x1, (b - 1) * TILES + (t + 1))
                else:
                    sp.wait_ge(s_cz, B)
                    sp.wait_ge(s_x[t], 16)
                sp.dma_start(xin[:, t, :], xnew[:, t, :]).then_inc(s_xin[t], 16)

            def store(b, t):
                if not exists(b):
                    return
                dst = out_v[b * TILES + t] if isinstance(b, int) else out_v[bass.ds(b * TILES + t, 1)].squeeze(0)
                sp.wait_ge(s_fin, b * (2 * TILES) + 2 * (t + 1))
                sp.dma_start(dst, zc[:, t, :]).then_inc(s_stored[t], 16)

            def round_(m):
                store(m - 2, 0)
                keep(m + 1, 0)
                store(m - 2, 1)
                store(m - 2, 2)
                load(m + 2, 0)
                keep(m + 1, 1)
                store(m - 2, 3)
                load(m + 2, 1)
                keep(m + 1, 2)
                load(m + 2, 2)
                keep(m + 1, 3)
                load(m + 2, 3)

            round_(-1)
            raw(6)
            round_(0)
            round_(1)
            with sp.Fori(2, STEADY) as m:
                round_(m)
            for m in range(STEADY, BLOCKS + 2):
                round_(m)
            for t in range(TILES):
                sp.wait_ge(s_stored[t], 16 * BLOCKS)

        @block.gpsimd
        def _(pool):
            pool.memset(ones[:], 1.0).then_inc(s_id, 1)
            pool.wait_ge(s_id, 1)
            pool.affine_select(out=ident[:], in_=ones[:], compare_op=ALU.is_equal, fill=0.0, base=0,
                               pattern=[[-1, P]], channel_multiplier=1).then_inc(s_id, 1)
            pool.memset(minus_half[:], -0.5).then_inc(s_clear, 1)
            pool.memset(eps[:], EPS).then_inc(s_clear, 1)
            pool.memset(zero[:], 0.0).then_inc(s_clear, 1)
            pool.wait_ge(s_clear, 3)

            def norm_steps(mean, var, r, sh, signal, before):
                n, w = var.shape
                pool.tensor_tensor(r, var, eps[0:n, 0:w], ALU.add).then_inc(signal, 1)
                pool.wait_ge(signal, before + 1)
                pool.tensor_tensor(r, r, minus_half[0:n, 0:w], ALU.pow).then_inc(signal, 1)
                pool.wait_ge(signal, before + 2)
                pool.tensor_tensor(sh, mean, r, ALU.mult).then_inc(signal, 1)
                pool.wait_ge(signal, before + 3)
                pool.tensor_tensor(sh, zero[0:n, 0:w], sh, ALU.subtract).then_inc(signal, 1)

            pool.wait_ge(s_cstat, 2 * B)
            norm_steps(mv[0:C, :, 0], mv[0:C, :, 1], rstd[0:C, :], shift[0:C, :], s_crs, 0)

            for l in LAYERS:
                pool.memset(v_all[l][:], 0.0).then_inc(s_clear, 1)
                pool.memset(k_now[l][:], 0.0).then_inc(s_clear, 1)
            ones_at = vst[0:C, :, :, HD].rearrange("p (b i) h -> p b i h", i=2)
            pool.memset(ones_at[:, :, HI, :], 1.0).then_inc(s_clear, 1)
            pool.memset(ones_at[:, :, LO, :], 0.0).then_inc(s_clear, 1)
            pool.wait_ge(s_fsplit, 4)
            for i in range(2):
                pool.memset(prob[i][:, UK:UP], 0.0).then_inc(s_clear, 1)

            def norm_columns(stats, r, sh, t, signal, before):
                norm_steps(stats[:, t, 0:1], stats[:, t, 1:2], r[:, t:t + 1], sh[:, t:t + 1], signal, before)

            def x_columns(b, t):
                if exists(b):
                    pool.wait_ge(s_stat, b * (2 * TILES) + 2 * (t + 1))
                    norm_columns(mv, rstd, shift, t, s_rs, b * (4 * TILES) + 4 * t)

            def last_columns(b, t):
                if exists(b):
                    pool.wait_ge(s_stat2, b * (2 * TILES) + 2 * (t + 1))
                    norm_columns(mv2, rstd2, shift2, t, s_rs2, b * (4 * TILES) + 4 * t)

            def add_x(b, t):
                if exists(b):
                    pool.wait_ge(s_xin[t], b * 16 + 16)
                    pool.wait_ge(s_norm, unit(0, b, 2 * t + 1))
                    pool.tensor_tensor(x1[:, t, :], x1[:, t, :], xin[:, t, :], ALU.add).then_inc(s_x1, 1)

            def bias_x1(b, t):
                if not exists(b):
                    return
                if isinstance(b, int) and b == 0:
                    pool.wait_ge(s_rows, 16 * 4)
                    pool.wait_ge(s_wlow, len(jobs))
                pool.wait_ge(s_x1, b * TILES + (t + 1))
                if exists(b - 1):
                    pool.wait_ge(s_low, MISC.done("wo", t, b - 1))
                pool.tensor_tensor(x1b[:, t, :], x1[:, t, :], rows_bc[:, 0, :], ALU.add).then_inc(s_x1b, 1)

            def finish(b, t):
                if not exists(b):
                    return
                n = b * (2 * TILES) + 2 * t
                r = zc[:, t, :]
                pool.wait_ge(s_applied, b * TILES + (t + 1))
                pool.tensor_tensor(r, r, rows_bc[:, 1, :], ALU.mult).then_inc(s_fin, 1)
                pool.wait_ge(s_fin, n + 1)
                pool.tensor_tensor(r, r, rows_bc[:, 2, :], ALU.add).then_inc(s_fin, 1)

            def round_(m):
                if isinstance(m, int) and m == BLOCKS + 1:
                    for t in range(1, TILES):
                        last_columns(m - 2, t)
                    return
                late = isinstance(m, int) and m == BLOCKS
                if is_int(m, 0):
                    for t in range(TILES):
                        x_columns(m + 1, t)
                bias_x1(m - 1, 1)
                if not late:
                    bias_x1(m - 1, 2)
                last_columns(m - 2, 1)
                add_x(m, 0)
                if late:
                    finish(m - 2, 1)
                    bias_x1(m - 1, 2)
                last_columns(m - 2, 2)
                if not late:
                    finish(m - 2, 1)
                bias_x1(m - 1, 3)
                last_columns(m - 2, 3)
                finish(m - 2, 2)
                add_x(m, 1)
                if not is_int(m, 0):
                    x_columns(m + 1, 3)
                finish(m - 2, 3)
                add_x(m, 2)
                add_x(m, 3)
                if not is_int(m, -1):
                    for t in range(3):
                        x_columns(m + 2, t)
                bias_x1(m, 0)
                last_columns(m - 1, 0)
                finish(m - 1, 0)

            for m in range(FIRST, 2):
                round_(m)
            with pool.Fori(2, STEADY) as m:
                round_(m)
            for m in range(STEADY, BLOCKS + 2):
                round_(m)

        def project(pe, dst, w, act, g, midway=lambda: None):
            n = 0
            for k in range(KC):
                if k == KC // 2:
                    midway()
                for a, b in ((HI, HI), (HI, LO), (LO, HI)):
                    mm = pe.matmul(dst, w[a][:, k, g * P:(g + 1) * P], act[b][:, k, :],
                                   start=(n == 0), stop=(n == 3 * KC - 1))
                    n += 1
            return mm

        @block.tensor
        def _(pe):
            pe.wait_ge(s_id, 2)
            for q, l in enumerate(LAYERS):
                pe.wait_ge(s_fsplit, 2 * (q + 1))
                pe.wait_ge(s_wlow, 2 * q + 1)
                for g in range(KC):
                    if q:
                        pe.wait_ge(s_kfull, g + 1)
                    project(pe, key_bank(g)[:, 0:BC], wk, fT[l], g).then_inc(s_kvmade, 1)
                if q == 0:
                    pe.wait_ge(s_cz, B)
                    for k in range(KC):
                        for b in range(B):
                            mm = pe.transpose(value_bank(k)[:, b * C:(b + 1) * C], zc[0:C, b, k * P:(k + 1) * P],
                                              ident[0:C, 0:C])
                        mm.then_inc(s_cturn, 1)
                pe.wait_ge(s_wlow, 2 * q + 2)
                for b in range(B):
                    if q:
                        pe.wait_ge(s_vfull, b + 1)
                    else:
                        pe.wait_ge(s_fn, b + 1)
                    n = 0
                    for k in range(KC):
                        for i, j in ((HI, HI), (HI, LO), (LO, HI)):
                            mm = pe.matmul(value_bank(b)[0:C, :], fT[l][i][:, k, b * C:(b + 1) * C], wv[j][:, k, :],
                                           start=(n == 0), stop=(n == 3 * KC - 1))
                            n += 1
                    mm.then_inc(s_kvmade, 1)
            pe.wait_ge(s_kfull, 2 * KC)

            def query_bias(g):
                if g == 0:
                    pe.wait_ge(s_cols, 16 * 6)
                    pe.wait_ge(s_wraw[0], 16 * 3)
                for k in range(KC):
                    mm = pe.matmul(key_bank(1)[:, g:g + 1], w_raw[0][:, k, g * P:(g + 1) * P], cols[:, BX, k:k + 1],
                                   start=(k == 0), stop=(k == KC - 1))
                mm.then_inc(s_bias0, 1)

            for g in range(KC):
                query_bias(g)

            turned_from = {"zT": zc, "xT": x1, "cT": zc}
            projections = {"qa": (w_q0, xT), "qb": (w_q1, xT)}

            def do_misc(m, layer, u, place, midway=lambda: None):
                item = item_at(m, layer, u, place)
                if item is None or item[0] in turned_from:
                    midway()
                if item is None:
                    return
                kind, t, b = item
                bank = bank_of(kind, t, b)
                if place == 1:
                    last, unit_before = last_in_bank(m, layer, u)
                    if last:
                        pe.wait_ge(s_low, MISC.done(*last))
                    elif unit_before:
                        pe.wait_ge(s_plow, 2 * unit(*unit_before))
                    elif isinstance(m, int) and m == -1:
                        pe.wait_ge(s_vfull, 2 * B)
                elif unit_at(m, layer, u + 1):
                    pe.wait_ge(s_sub, unit(*unit_at(m, layer, u + 1)))
                elif a_item_before(*step_before(m, layer, u)):
                    pe.wait_ge(s_low, MISC.done(*a_item_before(*step_before(m, layer, u))))
                made_from = {("qa", 0): ("zT", 3), ("qb", 0): ("xT", 3)}
                if kind == "wo":
                    pe.wait_ge(s_low, MISC.done("cT", t, b))
                elif kind == "qa" and isinstance(b, int) and b == 0 and t == 0:
                    pe.wait_ge(s_wlow, 5)
                if (kind, t) in made_from:
                    pe.wait_ge(s_low, MISC.done(*made_from[kind, t], b))
                if kind in turned_from:
                    src = turned_from[kind]
                    if kind == "zT":
                        pe.wait_ge(s_z[t], b * 16 + 16)
                    elif kind == "xT":
                        pe.wait_ge(s_x1, b * TILES + (t + 1))
                    else:
                        pe.wait_ge(s_norm, unit(1, b, 2 * t + 1))
                    for k in range(KC):
                        mm = pe.transpose(bank[:, k * P:(k + 1) * P], src[:, t, k * P:(k + 1) * P], ident[:])
                elif kind in projections:
                    if isinstance(b, int) and b == 0 and t == 0 and kind == "qb":
                        pe.wait_ge(s_wlow, 6)
                    w, act = projections[kind]
                    mm = project(pe, bank, w, act, t, midway)
                else:
                    if isinstance(b, int) and b == 0 and t == 0:
                        pe.wait_ge(s_wlow, 7)
                    n = 0
                    for k in range(KC):
                        if k == KC // 2:
                            midway()
                        for i, j in ((HI, HI), (HI, LO), (LO, HI)):
                            mm = pe.matmul(bank, cT[i][:, k, t * P:(t + 1) * P], w_o[j][:, k, :],
                                           start=(n == 0), stop=(n == 3 * KC - 1))
                            n += 1
                mm.then_inc(s_misc, 1)

            def make_scores(layer, b, u, in_bank):
                t, half = u // 2, u % 2
                n = unit(layer, b, u)
                if u < 2:
                    pe.wait_ge(s_low, MISC.done("qb" if layer else "qa", 2 * u + 1, b))
                    if u == 0:
                        pe.wait_ge(s_kv[layer], b * RENEWALS + GH)
                if not is_int(n, 2):
                    pe.wait_ge(s_sub, n - 2)
                q = qT[layer]
                if in_bank:
                    pe.wait_ge(s_low, MISC.done(*in_bank))
                for g in range(2):
                    for r, (i, j) in enumerate(((HI, HI), (HI, LO), (LO, HI))):
                        mm = pe.matmul(scores[:, half, g, 0:GK], q[i][:, 2 * half + g, t * P:(t + 1) * P],
                                       k_now[layer][:, j, 2 * half + g, :], start=(r == 0), stop=(r == 2))
                mm.then_inc(s_scores, 1)

            def turn_prob(layer, b, u):
                n = unit(layer, b, u)
                pe.wait_ge(s_exp, n)
                if not is_int(n, 1):
                    pe.wait_ge(s_plow, 2 * n - 2)
                for c in range(CH):
                    mm = pe.transpose(turned[:, c // 3, c % 3 * P:(c % 3 + 1) * P],
                                      prob[u % 2][:, c * P:(c + 1) * P], ident[:])
                    if c in (2, CH - 1):
                        mm.then_inc(s_turned, 1)

            def weigh_values(layer, b, u):
                n = unit(layer, b, u)
                if not is_int(n, 1):
                    pe.wait_ge(s_norm, n - 1)
                if u == 0:
                    pe.wait_ge(s_kv[layer], b * RENEWALS + RENEWALS)
                half, y = u % 2, heads_out
                pt = probT
                for c, (h0, h1, s) in enumerate(spans):
                    if c in (0, 3):
                        pe.wait_ge(s_plow, 2 * n - (1 if c == 0 else 0))
                    for i, j in ((HI, HI), (HI, LO), (LO, HI)):
                        mm = pe.matmul(y[:, h0 * VW:h1 * VW], pt[i][u % 2][:, c * P:(c + 1) * P],
                                       vnow(layer, j, half, s, h1 - h0),
                                       start=(c == 0 and i == HI and j == HI),
                                       stop=(c == CH - 1 and i == LO), skip_group_check=True)
                mm.then_inc(s_pv, 1)

            def round_(m):
                for layer in range(2):
                    for u in range(UNITS):
                        now, last, after_next = (unit_at(m, layer, u + i) for i in (0, -1, 2))
                        if now:
                            turn_prob(*now)
                        if last:
                            weigh_values(*last)
                        a_first = after_next and (layer, u) == (0, 7)
                        if a_first:
                            do_misc(m, layer, u, 0)
                        if after_next:
                            make_scores(*after_next, a_item_before(m, layer, u))
                        do_misc(m, layer, u, 1, midway=lambda: a_first or do_misc(m, layer, u, 0))

            for m in range(FIRST, 2):
                round_(m)
            with pe.Fori(2, STEADY) as m:
                round_(m)
            for m in range(STEADY, BLOCKS + 2):
                round_(m)

        targets = {"zT": xT, "xT": xT, "cT": cT}

        def high_low(kind, t, b, i):
            if kind in targets:
                return targets[kind][i][:, :, t * P:(t + 1) * P], bank_of(kind, t, b).rearrange("p (k r) -> p k r", k=KC)
            return qT[0 if kind == "qa" else 1][i][:, t, :], bank_of(kind, t, b)

        bias_col = {"qa": BQ0, "qb": BQ}

        @block.scalar
        def _(act):
            def weights_high(n):
                _, scale, (high, _low) = jobs[n]
                raw = w_raw[RAW[n]]
                act.wait_ge(s_wraw[RAW[n]], 16 * RAW[:n + 1].count(RAW[n]))
                if n in (2, 3, 5, 6):
                    act.wait_ge(s_kvmade, {2: KC, 3: 2 * KC, 5: 4 * KC, 6: 4 * KC}[n])
                if scale is None:
                    act.activation(high[:], raw[:], ACT.Copy).then_inc(s_whigh, 1)
                    return
                act.wait_ge(s_cols, 16 * 6)
                for k in range(KC):
                    ins = act.activation(high[:, k, :], raw[:, k, :], ACT.Copy, scale=cols[:, scale, k:k + 1])
                ins.then_inc(s_whigh, 1)

            def key_high(q, g):
                act.wait_ge(s_kfull, KC * q + g + 1)
                act.activation(k_all[LAYERS[q]][:, :, HI, g, :], kf[g % 2].rearrange("p (b c) -> p b c", b=B),
                               ACT.Copy).then_inc(s_khigh, 1)

            def value_high(q, b):
                act.wait_ge(s_vfull, B * q + b + 1)
                if q and not b:
                    act.wait_ge(s_place, 16 * len(places))
                act.activation(vst[0:C, 2 * b + HI, :, 0:HD], vf[b % 2][0:C, :].rearrange("p (h d) -> p h d", h=H),
                               ACT.Copy).then_inc(s_vhigh, 1)

            def normalise(b, t):
                if not exists(b):
                    return
                if isinstance(b, int) and b == 0:
                    act.wait_ge(s_cturn, KC)
                elif isinstance(b, int) and b <= 2:
                    act.wait_ge(s_misc, MISC.done("zT", t, b - 1))
                else:
                    act.wait_ge(s_stored[t], 16 * (b - 2))
                act.wait_ge(s_rs, b * (4 * TILES) + 4 * (t + 1))
                act.activation(zc[:, t, :], xnew[:, t, :], ACT.Identity, bias=shift[:, t:t + 1],
                               scale=rstd[:, t:t + 1]).then_inc(s_z[t], 16)

            weights_high(0)
            weights_high(1)
            act.wait_ge(s_crs, 4)
            for b in range(B):
                act.activation(zc[0:C, b, :], craw[0:C, b, :], ACT.Identity, bias=shift[0:C, b:b + 1],
                               scale=rstd[0:C, b:b + 1]).then_inc(s_cz, 1)
            for g in range(KC):
                key_high(0, g)
            weights_high(2)
            for b in range(B):
                value_high(0, b)
            weights_high(3)
            for g in range(KC):
                key_high(1, g)
            weights_high(4)
            for t in range(TILES):
                normalise(0, t)
            for b in range(B):
                value_high(1, b)

            def take_high(item):
                if item is None or item[0] == "wo":
                    return
                kind, t, b = item
                act.wait_ge(s_misc, MISC.done(kind, t, b))
                if kind == "qa" and isinstance(b, int) and b == 0 and t == 0:
                    act.wait_ge(s_bq0, 1)
                dst, src = high_low(kind, t, b, HI)
                if kind in bias_col:
                    act.activation(dst, src, ACT.Identity, bias=cols[:, bias_col[kind], t:t + 1]).then_inc(s_high, 1)
                else:
                    act.activation(dst, src, ACT.Copy).then_inc(s_high, 1)

            def apply_last(b, t):
                if not exists(b):
                    return
                act.wait_ge(s_rs2, b * (4 * TILES) + 4 * (t + 1))
                act.activation(zc[:, t, :], zc[:, t, :], ACT.Identity, bias=shift2[:, t:t + 1],
                               scale=rstd2[:, t:t + 1]).then_inc(s_applied, 1)

            def renew_kv(layer, b, part):
                if not exists(b):
                    return
                n = b // PER_BATCH
                if isinstance(b, int) and b == 0:
                    act.wait_ge(s_clear, 11)
                    act.wait_ge(s_klow, 2 * KC)
                    if part == GH:
                        act.wait_ge(s_place, 16 * len(places) * 2)
                elif part == 0:
                    act.wait_ge(s_scores, unit(layer, b - 1, UNITS - 1))
                elif part == GH:
                    act.wait_ge(s_pv, unit(layer, b - 1, UNITS - 1))
                a = k_all[layer] if part < GH else v_all[layer]
                src = a[:, n] if isinstance(n, int) else a[:, bass.ds(n, 1)].squeeze(1)
                if part < GH:
                    r = slice(part * HD, (part + 1) * HD)
                    act.activation(k_now[layer][r, :, :, part * C:(part + 1) * C], src[r], ACT.Copy)\
                       .then_inc(s_kv[layer], 1)
                else:
                    act.activation(v_now[layer][:], src, ACT.Copy).then_inc(s_kv[layer], 1)

            def exponent(layer, b, u):
                act.wait_ge(s_sub, unit(layer, b, u))
                p = prob[u % 2][:, 0:UK]
                act.activation(p, p, ACT.Exp).then_inc(s_exp, 1)

            def prob_high(layer, b, u):
                for part, (a, z) in enumerate(((0, 3 * P), (3 * P, UP))):
                    act.wait_ge(s_turned, 2 * unit(layer, b, u) - 1 + part)
                    act.activation(probT[HI][u % 2][:, a:z], turned[:, part, 0:z - a], ACT.Copy).then_inc(s_phigh, 1)

            def round_(m):
                for layer in range(2):
                    for u in range(UNITS):
                        now, ahead = (unit_at(m, layer, u + i) for i in (0, 1))
                        take_high(item_at(*step_before(m, layer, u), 1))
                        if now:
                            prob_high(*now)
                        if ahead:
                            exponent(*ahead)
                        at_b = item_at(m, layer, u, 1)
                        early = at_b is None or at_b[0] in targets
                        if early:
                            take_high(item_at(m, layer, u, 0))
                        if isinstance(m, int) and m == BLOCKS and (layer, u) in ((0, 3), (1, 2), (1, 3)):
                            apply_last(m - 2, 1 if layer == 0 else u)
                        elif isinstance(m, int) and m == BLOCKS + 1:
                            if layer == 0 and 2 <= u < 1 + TILES:
                                apply_last(m - 2, u - 1)
                        elif layer == 0 and u in (3, 4, 5) and not (isinstance(m, int) and m == BLOCKS):
                            apply_last(m - 2, u - 2)
                        if isinstance(m, int) and m == 0:
                            if layer == 0 and 1 <= u < 1 + TILES:
                                normalise(1, u - 1)
                        elif layer == 0 and u >= 5 and not is_int(m, -1):
                            for t in {5: (0,), 6: (1, 2), 7: (3,)}[u]:
                                normalise(m + 1, t)
                        if layer == 1 and u == 6:
                            apply_last(m - 1, 0)
                        if layer == 0:
                            for part in {0: (0,), 1: (1, 2), 2: (3,), 4: (4,)}.get(u, ()):
                                renew_kv(1, m - 1, part)
                        else:
                            for part in {0: (0,), 1: (1,), 2: (2, 3), 4: (4,)}.get(u, ()):
                                renew_kv(0, m + 1, part)
                        if not early:
                            take_high(item_at(m, layer, u, 0))
                        if isinstance(m, int) and (m, layer, u) == (-1, 1, 1):
                            weights_high(5)
                        if isinstance(m, int) and (m, layer, u) == (0, 1, 0):
                            weights_high(6)

            for m in range(FIRST, 2):
                round_(m)
            with act.Fori(2, STEADY) as m:
                round_(m)
            for m in range(STEADY, BLOCKS + 2):
                round_(m)

        @block.vector
        def _(dve):
            def split_context(q):
                high, low = fT[LAYERS[q]]
                dve.tensor_copy(high, fnT).then_inc(s_fsplit, 1)
                dve.wait_ge(s_fsplit, 2 * q + 1)
                dve.tensor_tensor(low, fnT, high.bitcast(F32), ALU.subtract).then_inc(s_fsplit, 1)

            def weights_low(n):
                _, scale, (high, low) = jobs[n]
                raw = w_raw[RAW[n]]
                dve.wait_ge(s_whigh, n + 1)
                if scale is None:
                    dve.tensor_tensor(low[:], raw[:], high[:].bitcast(F32), ALU.subtract).then_inc(s_wlow, 1)
                    return
                for k in range(KC):
                    ins = dve.scalar_tensor_tensor(low[:, k, :], raw[:, k, :], cols[:, scale, k:k + 1],
                                                   high[:, k, :].bitcast(F32), ALU.mult, ALU.subtract)
                ins.then_inc(s_wlow, 1)

            def key_full(q, g):
                n = KC * q + g + 1
                dve.wait_ge(s_kvmade, 2 * KC * q + g + 1)
                if n > 2:
                    dve.wait_ge(s_klow, n - 2)
                dve.tensor_scalar(kf[g % 2], key_bank(g)[:, 0:BC], SCALE, cols[:, BKS if LAYERS[q] else ZERO, g:g + 1],
                                  ALU.mult, ALU.add).then_inc(s_kfull, 1)

            def key_low(q, g):
                n = KC * q + g + 1
                dve.wait_ge(s_kfull, n)
                dve.wait_ge(s_khigh, n)
                k = k_all[LAYERS[q]]
                dve.tensor_tensor(k[:, :, LO, g, :], kf[g % 2].rearrange("p (b c) -> p b c", b=B), k[:, :, HI, g, :],
                                  ALU.subtract).then_inc(s_klow, 1)

            def value_full(q, b):
                n = B * q + b + 1
                dve.wait_ge(s_kvmade, 2 * KC * q + KC + b + 1)
                if n > 2:
                    dve.wait_ge(s_vlow, n - 2)
                if LAYERS[q]:
                    dve.wait_ge(s_rows, 16)
                    dve.tensor_tensor(vf[b % 2][0:C, :], value_bank(b)[0:C, :], bv_bc[0:C, :],
                                      ALU.add).then_inc(s_vfull, 1)
                else:
                    dve.tensor_copy(vf[b % 2][0:C, :], value_bank(b)[0:C, :]).then_inc(s_vfull, 1)

            def value_low(q, b):
                n = B * q + b + 1
                dve.wait_ge(s_vfull, n)
                dve.wait_ge(s_vhigh, n)
                dve.tensor_tensor(vst[0:C, 2 * b + LO, :, 0:HD], vf[b % 2][0:C, :].rearrange("p (h d) -> p h d", h=H),
                                  vst[0:C, 2 * b + HI, :, 0:HD], ALU.subtract).then_inc(s_vlow, 1)

            def split_all(q, full, low):
                full(q, 0)
                for i in range(1, 4):
                    full(q, i)
                    low(q, i - 1)
                low(q, 3)

            def x_stats(b, t):
                dve.wait_ge(s_x[t], b * 16 + 16)
                if exists(b - 1):
                    dve.wait_ge(s_z[t], b * 16)
                elif t == 0:
                    dve.wait_ge(s_cz, B)
                dve.bn_stats(stat[:, t, :], xnew[:, t, :]).then_inc(s_stat, 1)

            def x_aggr(b, t):
                dve.wait_ge(s_stat, b * (2 * TILES) + (2 * t + 1))
                dve.memset(idle_dve[:], 0.0)
                dve.bn_aggr(mv[:, t, :], stat[:, t, :]).then_inc(s_stat, 1)

            dve.wait_ge(s_ctxT, 16)
            split_context(0)
            weights_low(0)
            dve.wait_ge(s_ctx, 16)
            for b in range(B):
                dve.bn_stats(stat[0:C, b, :], craw[0:C, b, :]).then_inc(s_cstat, 1)
                dve.wait_ge(s_cstat, 2 * b + 1)
                dve.bn_aggr(mv[0:C, b, :], stat[0:C, b, :]).then_inc(s_cstat, 1)
            weights_low(1)
            dve.wait_ge(s_cols, 16 * 6)
            dve.tensor_scalar(cols[:, BKS, :], cols[:, BK, :], SCALE, None, ALU.mult).then_inc(s_bks, 1)
            dve.memset(cols[:, ZERO, :], 0.0).then_inc(s_bks, 1)
            dve.wait_ge(s_bks, 2)
            dve.wait_ge(s_fsplit, 2)
            for k in range(KC):
                dve.wait_ge(s_cturn, k + 1)
                dve.tensor_scalar(fnT[:, k, :], value_bank(k)[:, 0:BC], cols[:, GF, k:k + 1], cols[:, BF, k:k + 1],
                                  ALU.mult, ALU.add).then_inc(s_fn, 1)
            split_all(0, key_full, key_low)
            dve.wait_ge(s_fn, KC)
            split_context(1)
            weights_low(2)
            split_all(0, value_full, value_low)
            weights_low(3)
            split_all(1, key_full, key_low)
            for t in range(TILES):
                x_stats(0, t)
                x_aggr(0, t)
            weights_low(4)
            split_all(1, value_full, value_low)

            def take_low(item):
                if item is None:
                    return
                kind, t, b = item
                if kind == "wo":
                    dve.wait_ge(s_misc, MISC.done(kind, t, b))
                    dve.wait_ge(s_x1b, b * TILES + (t + 1))
                    dve.tensor_tensor(zc[:, t, :], bank_of(kind, t, b), x1b[:, t, :], ALU.add).then_inc(s_low, 1)
                    return
                dve.wait_ge(s_high, SPLIT.done(kind, t, b))
                dst, src = high_low(kind, t, b, LO)
                high, _ = high_low(kind, t, b, HI)
                if kind in bias_col:
                    dve.scalar_tensor_tensor(dst, src, cols[:, bias_col[kind], t:t + 1], high, ALU.add,
                                             ALU.subtract).then_inc(s_low, 1)
                else:
                    dve.tensor_tensor(dst, src, high.bitcast(F32), ALU.subtract).then_inc(s_low, 1)

            def last_stats(b, t):
                dve.wait_ge(s_low, MISC.done("wo", t, b))
                dve.bn_stats(stat2[:, t, :], zc[:, t, :]).then_inc(s_stat2, 1)

            def last_aggr(b, t):
                dve.wait_ge(s_stat2, b * (2 * TILES) + (2 * t + 1))
                dve.memset(idle_dve[:], 0.0)
                dve.bn_aggr(mv2[:, t, :], stat2[:, t, :]).then_inc(s_stat2, 1)

            def seen_scores(u):
                return scores[:, u % 2, :, 0:GK].rearrange("p g (h c) -> p g h c", c=C), \
                    top[:, u % 2, :].rearrange("p (g h) -> p g h", g=2)

            def find_top(layer, b, u):
                s, mx = seen_scores(u)
                dve.wait_ge(s_scores, unit(layer, b, u))
                dve.tensor_reduce(mx, s, AX.X, ALU.max).then_inc(s_top, 1)

            def subtract_top(layer, b, u):
                n = unit(layer, b, u)
                s, mx = seen_scores(u)
                dve.wait_ge(s_top, n)
                if not is_int(n, 2):
                    dve.wait_ge(s_turned, 2 * n - 4)
                dve.tensor_tensor(prob[u % 2][:, 0:UK].rearrange("p (g h c) -> p g h c", g=2, c=C), s,
                                  mx.unsqueeze(3).to_broadcast([P, 2, GH, C]),
                                  ALU.subtract).then_inc(s_sub, 1)

            def prob_low(layer, b, u, part):
                a, z = ((0, 3 * P), (3 * P, UP))[part]
                dve.wait_ge(s_phigh, 2 * unit(layer, b, u) - 1 + part)
                dve.tensor_tensor(probT[LO][u % 2][:, a:z], turned[:, part, 0:z - a], probT[HI][u % 2][:, a:z],
                                  ALU.subtract).then_inc(s_plow, 1)

            y = heads_out[:, 0:8 * VW].rearrange("p (h v) -> p h v", v=VW)

            def invert(layer, b, u):
                dve.wait_ge(s_pv, unit(layer, b, u))
                dve.reciprocal(rden[:, u % 2, :], y[:, :, HD]).then_inc(s_rden, 1)

            def norm_heads(layer, b, u):
                t, half = u // 2, u % 2
                dve.wait_ge(s_rden, unit(layer, b, u))
                to = (x1, zc)[layer][:, t, half * (D // 2):(half + 1) * (D // 2)]
                if layer == 0 and exists(b - 1):
                    dve.wait_ge(s_x1b, (b - 1) * TILES + (t + 1))
                if layer == 1:
                    if exists(b + 2):
                        dve.wait_ge(s_misc, MISC.done("zT", t, b + 2))
                    else:
                        dve.wait_ge(s_stored[t], 16 * b)
                dve.tensor_tensor(to.rearrange("p (h d) -> p h d", d=HD), y[:, :, 0:HD],
                                  rden[:, u % 2, :].unsqueeze(2).to_broadcast([P, 8, HD]),
                                  ALU.mult).then_inc(s_norm, 1)

            def stats_at(m, layer, u):
                if isinstance(m, int) and m == 0 and layer == 0:
                    return (x_stats, x_aggr, 1, u) if u < TILES else None
                if isinstance(m, int) and m == BLOCKS + 1:
                    return (last_stats, last_aggr, m - 2, u) if layer == 0 and 1 <= u < TILES else None
                if isinstance(m, int) and m == BLOCKS and layer == 0 and u > 2:
                    return None
                if isinstance(m, int) and m == BLOCKS and layer == 1 and u in (1, 2):
                    return last_stats, last_aggr, m - 2, u + 1
                if layer == 0 and u in (2, 3, 4):
                    at = last_stats, last_aggr, m - 2, u - 1
                elif layer == 0 and u == 5:
                    at = x_stats, x_aggr, m + 1, 3
                elif layer == 1 and u in (1, 2, 4):
                    at = x_stats, x_aggr, m + 2, {1: 0, 2: 1, 4: 2}[u]
                elif layer == 1 and u == 5:
                    at = last_stats, last_aggr, m - 1, 0
                else:
                    return None
                if not exists(at[2]) or is_int(m, -1):
                    return None
                return at

            def round_(m):
                for layer in range(2):
                    for u in range(UNITS):
                        now, last, ahead = (unit_at(m, layer, u + i) for i in (0, -1, 1))
                        if ahead:
                            find_top(*ahead)
                        take_low(item_at(*step_before(m, layer, u), 0))
                        if ahead:
                            subtract_top(*ahead)
                        take_low(item_at(*step_before(m, layer, u), 1))
                        if now:
                            prob_low(*now, 0)
                        if last:
                            invert(*last)
                        if now:
                            prob_low(*now, 1)
                        stats = stats_at(m, layer, u)
                        if stats:
                            first_part, second_part, b, t = stats
                            first_part(b, t)
                        if last:
                            norm_heads(*last)
                        if stats:
                            second_part(b, t)
                        if isinstance(m, int) and m == -1 and layer == 1 and u == 0:
                            dve.wait_ge(s_bias0, KC)
                            dve.tensor_copy(cols[:, BQ0, :], key_bank(1)[:, 0:KC]).then_inc(s_bq0, 1)
                            dve.wait_ge(s_bq0, 1)
                        if isinstance(m, int) and (m, layer, u) == (-1, 1, 1):
                            weights_low(5)
                        if isinstance(m, int) and (m, layer, u) == (0, 1, 0):
                            weights_low(6)

            for m in range(FIRST, 2):
                round_(m)
            with dve.Fori(2, STEADY) as m:
                round_(m)
            for m in range(STEADY, BLOCKS + 2):
                round_(m)

            for t in range(1, TILES):
                n = 2 * TILES * (BLOCKS - 1) + 2 * t
                r = zc[:, t, :]
                dve.wait_ge(s_applied, (BLOCKS - 1) * TILES + (t + 1))
                if t == 1:
                    dve.wait_ge(s_fin, n)
                dve.tensor_tensor(r, r, rows_bc[:, 1, :], ALU.mult).then_inc(s_fin, 1)
                dve.wait_ge(s_fin, n + 1)
                dve.tensor_tensor(r, r, rows_bc[:, 2, :], ALU.add).then_inc(s_fin, 1)


_OUT = ((4, 2048, 512), "float32")


def kernel(x, ctx_1024, L0_xattn_Wq, L0_xattn_Wk, L0_xattn_Wv, L0_xattn_gamma_x, L0_xattn_beta_x,
           L0_xattn_gamma_f, L0_xattn_beta_f, L1_xattn_W_qkv, L1_xattn_b_qkv, L1_xattn_W_o, L1_xattn_b_o,
           L1_xattn_ln_gamma, L1_xattn_ln_beta):
    import concourse.bacc as bacc
    from concourse.bass_utils import run_bass_kernel_spmd

    def column(v):
        return np.ascontiguousarray(np.asarray(v).reshape(4, 128).T)

    c = np.asarray(ctx_1024)
    b = np.asarray(L1_xattn_b_qkv)
    arrays = {
        "x": np.asarray(x), "ctx_rows": c,
        "ctx_turned": np.ascontiguousarray(c.reshape(-1, c.shape[-1]).T),
        "wq0": np.asarray(L0_xattn_Wq), "wk0": np.asarray(L0_xattn_Wk), "wv0": np.asarray(L0_xattn_Wv),
        "gx": column(L0_xattn_gamma_x), "bx": column(L0_xattn_beta_x),
        "gf": column(L0_xattn_gamma_f), "bf": column(L0_xattn_beta_f),
        "w1_turned": np.ascontiguousarray(np.asarray(L1_xattn_W_qkv).T),
        "bq1": column(b[0:512]), "bk1": column(b[512:1024]), "bv1": np.ascontiguousarray(b[1024:1536]),
        "wo_turned": np.ascontiguousarray(np.asarray(L1_xattn_W_o).T),
        "bo": np.asarray(L1_xattn_b_o), "ln_gamma": np.asarray(L1_xattn_ln_gamma),
        "ln_beta": np.asarray(L1_xattn_ln_beta),
    }
    nc = bacc.Bacc("TRN2", target_bir_lowering=False, num_devices=1)
    args = [nc.dram_tensor(n, a.shape, mybir.dt.from_np(a.dtype), kind="ExternalInput").ap()
            for n, a in arrays.items()]
    out = nc.dram_tensor("result", _OUT[0], F32, kind="ExternalOutput").ap()
    build(nc, *args, out)
    return run_bass_kernel_spmd(nc, [arrays], core_ids=[0]).results[0]["result"]
```
